# Optimizing a Trainium2 kernel written in Bass

```python
import numpy as np
import jax
import jax.numpy as jnp

def _softmax(x, axis=-1):
    return jax.nn.softmax(x, axis=axis)

def _gelu(x):
    return jax.nn.gelu(x, approximate=True)

def _silu(x):
    return jax.nn.silu(x)

def _sigmoid(x):
    return jax.nn.sigmoid(x)

def _layernorm(x, axis=-1, eps=1e-05):
    m = jnp.mean(x, axis=axis, keepdims=True)
    v = jnp.var(x, axis=axis, keepdims=True)
    return (x - m) / jnp.sqrt(v + eps)

def _scatter_add(tgt, idx, src, axis=0):
    return tgt.at[idx].add(src)

def _segment_sum(src, seg, n):
    return jax.ops.segment_sum(src, seg, n)
kernel_name = 'mk_seq_postln_d1_jaxref_r4_e8e808'

def setup_inputs(seed: int=0):
    np.random.seed(seed)
    _w = jnp.asarray

    def _L0_attn_setup():
        import jax, jax.numpy as jnp
        import numpy as np
        N_EMBD = 256
        N_HEAD = 16
        HEAD_SIZE = 64
        LN_EPS = 0.001
        key = jax.random.key(seed)
        ks = jax.random.split(key, 7)
        B, S, D, H, E = (4, 512, N_EMBD, N_HEAD, HEAD_SIZE)
        x = jax.random.normal(ks[0], (B, S, D), dtype=jnp.float32)
        scale = 1.0 / np.sqrt(D)
        Wq = jax.random.normal(ks[1], (H, D, E), dtype=jnp.float32) * scale
        Wk = jax.random.normal(ks[2], (H, D, E), dtype=jnp.float32) * scale
        Wv = jax.random.normal(ks[3], (H, D, E), dtype=jnp.float32) * scale
        Wo = jax.random.normal(ks[4], (H * E, D), dtype=jnp.float32) * scale
        gamma = jnp.ones((D,), dtype=jnp.float32)
        beta = jnp.zeros((D,), dtype=jnp.float32)
        return {'x': x, 'Wq': Wq, 'Wk': Wk, 'Wv': Wv, 'Wo': Wo, 'gamma': gamma, 'beta': beta}
    _L0_attn_in = _L0_attn_setup()

    def _L0_ffn_setup():
        import jax, jax.numpy as jnp
        import numpy as np
        DIM = 256
        HIDDEN = 768
        SCALE = 1.0 / 127.0

        def _dequant(w_int, dtype):
            return w_int.astype(dtype) * jnp.asarray(SCALE, dtype)
        key = jax.random.key(seed)
        k_x, k_g, k_u, k_d = jax.random.split(key, 4)
        x = jax.random.normal(k_x, (4, 512, DIM), dtype=jnp.float32)
        w_gate = jax.random.randint(k_g, (HIDDEN, DIM), -127, 128, dtype=jnp.int32)
        w_up = jax.random.randint(k_u, (HIDDEN, DIM), -127, 128, dtype=jnp.int32)
        w_down = jax.random.randint(k_d, (DIM, HIDDEN), -127, 128, dtype=jnp.int32)
        return {'x': x, 'w_gate': w_gate, 'w_up': w_up, 'w_down': w_down}
    _L0_ffn_in = _L0_ffn_setup()
    _d = {'L0_attn_x': _L0_attn_in['x'], 'L0_attn_Wq': _L0_attn_in['Wq'], 'L0_attn_Wk': _L0_attn_in['Wk'], 'L0_attn_Wv': _L0_attn_in['Wv'], 'L0_attn_Wo': _L0_attn_in['Wo'], 'L0_attn_gamma': _L0_attn_in['gamma'], 'L0_attn_beta': _L0_attn_in['beta'], 'L0_ffn_w_gate': _L0_ffn_in['w_gate'], 'L0_ffn_w_up': _L0_ffn_in['w_up'], 'L0_ffn_w_down': _L0_ffn_in['w_down']}
    _x0 = _d['L0_attn_x']
    _d['L0_attn_x'] = jax.random.normal(jax.random.fold_in(jax.random.key(seed), 1), (4, 1024, 256), dtype=_x0.dtype)
    del _x0
    return _d

def reference(L0_attn_x, L0_attn_Wq, L0_attn_Wk, L0_attn_Wv, L0_attn_Wo, L0_attn_gamma, L0_attn_beta, L0_ffn_w_gate, L0_ffn_w_up, L0_ffn_w_down):

    def _L0_attn_ref(x, Wq, Wk, Wv, Wo, gamma, beta):
        import jax, jax.numpy as jnp
        import numpy as np
        N_EMBD = 256
        N_HEAD = 16
        HEAD_SIZE = 64
        LN_EPS = 0.001
        B, S, D = x.shape
        H, _, E = Wq.shape
        q = jnp.einsum('bsd,hde->bhse', x, Wq)
        k = jnp.einsum('bsd,hde->bhse', x, Wk)
        v = jnp.einsum('bsd,hde->bhse', x, Wv)
        scores = jnp.einsum('bhse,bhte->bhst', q, k)
        causal = jnp.tril(jnp.ones((S, S), dtype=bool))
        scores = jnp.where(causal, scores / jnp.sqrt(jnp.float32(E)), jnp.float32(-jnp.inf))
        attn = jax.nn.softmax(scores, axis=-1)
        out = jnp.einsum('bhst,bhte->bhse', attn, v)
        heads = out.transpose(0, 2, 1, 3).reshape(B, S, H * E)
        y = x + heads @ Wo
        mu = jnp.mean(y, axis=-1, keepdims=True)
        var = jnp.mean(jnp.square(y - mu), axis=-1, keepdims=True)
        y = (y - mu) * jax.lax.rsqrt(var + LN_EPS) * gamma + beta
        return y

    def _L0_ffn_ref(x, w_gate, w_up, w_down):
        import jax, jax.numpy as jnp
        import numpy as np
        DIM = 256
        HIDDEN = 768
        SCALE = 1.0 / 127.0

        def _dequant(w_int, dtype):
            return w_int.astype(dtype) * jnp.asarray(SCALE, dtype)
        wg = _dequant(w_gate, x.dtype)
        wu = _dequant(w_up, x.dtype)
        wd = _dequant(w_down, x.dtype)
        gate = jnp.einsum('bsd,hd->bsh', x, wg)
        up = jnp.einsum('bsd,hd->bsh', x, wu)
        h = jax.nn.silu(gate) * up
        return jnp.einsum('bsh,dh->bsd', h, wd)
    x = L0_attn_x
    x = _layernorm(x + _L0_attn_ref(x, L0_attn_Wq, L0_attn_Wk, L0_attn_Wv, L0_attn_Wo, L0_attn_gamma, L0_attn_beta), axis=-1)
    x = _layernorm(x + _L0_ffn_ref(x, L0_ffn_w_gate, L0_ffn_w_up, L0_ffn_w_down), axis=-1)
    return x

_drawn_inputs = setup_inputs


def setup_inputs(seed=0):
    import zlib

    import numpy as np

    out = dict(_drawn_inputs(seed))
    spreads = {'L0_attn_gamma': (1.0, 0.2), 'L0_attn_beta': (0.0, 0.1)}
    factors = {}
    for name, (base, spread) in spreads.items():
        noise = np.random.default_rng([zlib.crc32(name.encode()), seed]).standard_normal(out[name].shape)
        drawn = base * np.exp(spread * noise) if base else spread * noise
        out[name] = jnp.asarray(drawn.astype(out[name].dtype))
    for name, factor in factors.items():
        out[name] = (out[name] * factor).astype(out[name].dtype)
    return out
```

```python
import concourse.bass as bass
from concourse import mybir
from contextlib import ExitStack

F32 = mybir.dt.float32
F32R = mybir.dt.float32r
BF16 = mybir.dt.bfloat16
I32 = mybir.dt.int32
ALU = mybir.AluOpType
ACT = mybir.ActivationFunctionType
AX = mybir.AxisListType

P = 128
B, S, D = 4, 1024, 256
H, E = 16, 64
HID = 768
KD = D // P
QH = 4
NQ = H // QH
NIT = B * NQ
TT = S // P
CH = 512
NH6 = HID // P
LN_EPS_ATTN = 1e-3
LN_EPS = 1e-5
SCALE = float(E) ** -0.5
WSCALE = 1.0 / 127.0
MASKED = -1e30

STEPS = [(i, c) for c in range(S // CH) for i in range(4 * (c + 1))]
NS = len(STEPS)
NST = QH * NS
CHUNKS = [(j, c) for j in range(TT) for c in range(j // 4 + 1)]
NC = len(CHUNKS)
NMX = QH * (NC + 1)
LAG = 3
RING = 3


def step_cols(i, c):
    lo = max(0, P * i - CH * c)
    return min(lo, CH - 2 * P), lo


RING_ORDER = ([("c", 0, k) for k in range(NC)] + [("c", 1, k) for k in range(6)] + [("t", 0, 0)]
              + [("c", 1, k) for k in range(6, NC)] + [("t", 1, 0)]
              + [("c", 2, k) for k in range(NC)] + [("c", 3, k) for k in range(3)] + [("t", 2, 0)]
              + [("c", 3, k) for k in range(3, NC)] + [("t", 3, 0)])
RING_AT = {e: n for n, e in enumerate(RING_ORDER)}

STAGE_AT = [2, 4, 6, 8]
MAXT_AT = {14: 2, 26: 3}
COPY_AT = {12 * n + 7: (n, 0) for n in range(QH)} | {12 * n + 15: (n, 1) for n in range(QH - 1)}
RECIP_AT = {12 * n + 20: n for n in range(QH - 1)}
NORM_AT = {40: 0}
T_LN1, T_LN1R, T_LN1N, T_AFF, T_ADD, T_LN2R, T_X1 = 13, 14, 15, 16, 17, 18, 20
T_TR, T_X1S = 22, 23
T_UP, T_GATE, T_HS, T_HL, T_DOWN = [25, 29, 33], [26, 30, 34], [27, 31, 35], [28, 32, 36], [31, 35, 39]
T_Y2, T_LN3R, T_OUT = 41, 42, 43


def build(nc, xT, x, wqkv, wo, wg, wu, wd, gamma, beta, out, yscr, rscr):
    ctx = ExitStack()
    with ctx:
        def sb(name, shape, dt=F32):
            return ctx.enter_context(nc.sbuf_tensor(name, shape, dt))

        def sem(name):
            return ctx.enter_context(nc.semaphore(name))

        raw = sb("raw", [P, S])
        xh, xl = sb("xh", [P, KD, S], F32R), sb("xl", [P, KD, S], F32R)
        WC = 3 * QH * E
        wh, wl = sb("wh", [P, KD, WC], F32R), sb("wl", [P, KD, WC], F32R)
        Q1, Q2 = sb("Q1", [P, QH, S], F32R), sb("Q2", [P, QH, S], F32R)
        K1, K2 = sb("K1", [P, QH, S], F32R), sb("K2", [P, QH, S], F32R)
        VW = 3 * E
        VH, VL = sb("VH", [P, TT, 2, VW], F32R), sb("VL", [P, TT, 2, VW], F32R)
        pe_ = sb("probs", [P, 2, CH])
        ph, pl = sb("probs_hi", [P, RING, CH], F32R), sb("probs_lo", [P, RING, CH], F32R)
        HT = sb("heads_T", [P, 2, S])
        rsum = sb("row_sums", [P, S])
        RB = sb("recip_bc", [P, S])
        S64, R64 = sb("sums64", [E, S // E]), sb("recip64", [E, S // E])
        mp = sb("max_part", [P, 2, NC])
        M8 = sb("neg_max8", [TT, 2, P], F32R)
        WoS = sb("wo_quad", [P, 2, D])
        y = sb("y", [P, TT, D])
        Wg, Wu, Wd = sb("w_gate", [P, KD, HID], F32R), sb("w_up", [P, KD, HID], F32R), sb("w_down", [P, NH6, D], F32R)
        yt, xt = sb("y_tail", [P, 2, D]), sb("x_tail", [P, 2, D])
        x1h, x1l = sb("x1T_hi", [P, KD, 2 * P], F32R), sb("x1T_lo", [P, KD, 2 * P], F32R)
        th, hh, hl = sb("tanh_h", [P, 2, 2 * P]), sb("h_hi", [P, 2, 2 * P], F32R), sb("h_lo", [P, 2, 2 * P], F32R)
        gm, bt = sb("gamma_bc", [P, D]), sb("beta_bc", [P, D])
        st, mv, rs = sb("bn_st", [P, 2, 6]), sb("mean_var", [P, 2, 2]), sb("rstd", [P, 2])
        halves, eps_attn, eps_ln = sb("minus_half", [P, 2]), sb("eps_attn", [P, 2]), sb("eps_ln", [P, 2])
        carrier = sb("carrier", [1, 1])
        identf, identb = sb("ident_f", [P, P]), sb("ident_b", [P, P], BF16)
        maskS = sb("mask_keys_free", [P, P], BF16)
        maskT = sb("mask_queries_free", [P, 2 * P], BF16)
        mraw = th[:, :, :].rearrange("p a b -> p (a b)")

        bank = [ctx.enter_context(nc.psum_tensor(f"bank{i}", [P, CH], F32)) for i in range(8)]
        misc, mxb, stb, pvb = bank[0:2], bank[2:4], bank[4:6], bank[6:8]

        raw_loaded = sem("raw_loaded")
        qk_dup = [sem("qk_dup0"), sem("qk_dup1")]
        max_row = [sem(f"max_row{n}") for n in range(QH)]
        sums_loaded, recip_stored, recip_bc = sem("sums_loaded"), sem("recip_stored"), sem("recip_bc_loaded")
        wo_loaded, y_stored, y_inited = sem("wo_loaded"), sem("y_stored"), sem("y_inited")
        tail_loaded, out_stored = sem("tail_loaded"), sem("out_stored")
        ffn_raw, consts_loaded = sem("ffn_raw_loaded"), sem("consts_loaded")
        const_step, const_b = sem("const_step"), sem("const_bf16")
        buf_init = sem("buffers_initialised")
        ffn_w = sem("ffn_weights_ready")
        raw_hi, raw_split = sem("raw_hi_done"), sem("raw_split_done")
        proj_mm, proj_hi, proj_lo = sem("proj_mm"), sem("proj_hi"), sem("proj_lo")
        v_mm, v_hi, v_lo = sem("v_mm"), sem("v_hi"), sem("v_lo")
        mx_mm, mx_read, mx_comb = sem("max_scores"), sem("max_read"), sem("max_combined")
        st_mm, exp_done, hi_done, lo_done, pv_mm = sem("scores_mm"), sem("exp_done"), sem("probs_hi_done"), sem("probs_lo_done"), sem("pv_mm")
        ht_copied, recip_done, ht_norm = sem("heads_copied"), sem("recip_done"), sem("heads_normed")
        wo_mm, y_added = sem("wo_mm"), sem("y_added")
        tdve, tpool, tact, tpe = sem("tail_dve"), sem("tail_pool"), sem("tail_act"), sem("tail_pe")

        def started(v):
            assert isinstance(v, int) or v.min_val > 0, "a register's value has to be positive"
            return not isinstance(v, int) or v > 0

        DV = {k: n + 1 for n, k in enumerate(
            ["st1a", "st1b", "mv1a", "mv1b", "n1a", "n1b", "add", "st2a", "st2b", "mv2a", "mv2b", "x1a", "x1b", "x1lo"]
            + [f"{k}{r}" for r in range(3) for k in ("tg", "h")]
            + ["y2a", "y2b", "st3a", "st3b", "mv3a", "mv3b", "oa", "ob"])}
        PL = {k: n + 1 for n, k in enumerate(
            ["xb", "e1", "r1", "gam", "e2", "r2", "hl0", "hl1", "hl2", "e3", "r3"])}
        AC = {k: n + 1 for n, k in enumerate(["x1hi", "tanh0", "hh0", "tanh1", "hh1", "tanh2", "hh2"])}
        PEC = {k: n + 1 for n, k in enumerate(["tr", "g0", "u0", "d0", "g1", "u1", "d1", "g2", "u2", "d2"])}
        ND, NP, NA, NPE = len(DV), len(PL), len(AC), len(PEC)

        block = ctx.enter_context(nc.Block())

        @block.sync
        def _(sp):
            def bits(ap):
                return ap.bitcast(F32)

            def load_piece(nxt, p, seq_b, quad):
                if started(4 * nxt + p):
                    sp.wait_ge(raw_split, 4 * nxt + p)
                if not isinstance(nxt, int):
                    sp.wait_ge(raw_loaded, 1)
                if p < KD:
                    src = xT[bass.ds(seq_b, 1), p, :, :].rearrange("o p n -> (o p) n")
                    sp.dma_start(raw[:, :], src).then_inc(raw_loaded, 16)
                else:
                    src = wqkv[bass.ds(quad, 1), p - KD, :, :].rearrange("o p n -> (o p) n")
                    sp.dma_start(raw[:, 0:WC], src).then_inc(raw_loaded, 16)

            def dup(it, pair):
                a, b = 2 * pair, 2 * pair + 1
                sp.wait_ge(proj_hi, 16 * it + 8 * pair + 4)
                sp.dma_start(bits(Q1[E:P, a, :]), bits(Q1[0:E, a, :])).then_inc(qk_dup[pair], 16)
                sp.dma_start(bits(Q1[0:E, b, :]), bits(Q1[E:P, b, :])).then_inc(qk_dup[pair], 16)
                sp.wait_ge(proj_hi, 16 * it + 8 * pair + 8)
                sp.dma_start(bits(K2[0:E, a, :]), bits(K1[0:E, a, :])).then_inc(qk_dup[pair], 16)
                sp.dma_start(bits(K2[E:P, b, :]), bits(K1[E:P, b, :])).then_inc(qk_dup[pair], 16)

            def max_to_row(it, n):
                if isinstance(it, int) and it == 0:
                    sp.wait_ge(buf_init, 14)
                sp.wait_ge(mx_read, NMX * it + RING_AT["t", n, 0] + 1)
                row = E if n % 2 == 0 else 0
                sp.dma_start(bits(Q2[row:row + 1, n, :]).rearrange("o (j q) -> o j q", j=TT), bits(M8[:, n % 2, :]))\
                    .then_inc(max_row[n], 16)

            def sums(it, n):
                sp.wait_ge(ht_copied, 2 * QH * it + 2 * n + 2)
                row = E if n % 2 == 0 else 0
                sp.dma_start(S64[:, :], rsum[row:row + 1, :].rearrange("o (a b) -> o a b", a=E)).then_inc(sums_loaded, 16)

            def recips(it, n):
                k = QH * it + n
                sp.wait_ge(recip_done, k + 1)
                sp.dma_start(rscr[n:n + 1, :].rearrange("o (a b) -> (o a) b", a=E), R64[:, :]).then_inc(recip_stored, 16)
                sp.wait_ge(recip_stored, 16 * (k + 1))
                rows = slice(0, E) if n % 2 == 0 else slice(E, P)
                sp.dma_start(RB[rows, :], rscr[n:n + 1, :].partition_broadcast(E).rearrange("e o n -> e (o n)")
                             ).then_inc(recip_bc, 16)

            def y_turn(b):
                if not (isinstance(b, int) and b == 0):
                    sp.wait_ge(y_added, 16 * b)
                    sp.wait_ge(raw_loaded, 1)
                    sp.dma_start(yscr.rearrange("(t p) d -> p t d", p=P), y[:, :, :]).then_inc(y_stored, 16)
                    sp.wait_ge(y_stored, 16 * b)
                    sp.wait_ge(raw_loaded, 1)
                if not (isinstance(b, int) and b == B):
                    src = x[bass.ds(b, 1), :, :].rearrange("o (t p) d -> p (o t) d", p=P)
                    sp.dma_start(y[:, :, :], src).then_inc(y_inited, 16)

            def tail_load(tt, b, j):
                sp.wait_ge(out_stored, 16 * (tt + 1))
                sp.wait_ge(raw_loaded, 1)
                sp.dma_start(yt[:, :, :], yscr.rearrange("(j t p) d -> j p t d", p=P, t=2)[bass.ds(j, 1)]
                             .rearrange("o p t d -> (o p) t d")).then_inc(tail_loaded, 16)
                src = x[bass.ds(b, 1), :, :].rearrange("o (j t p) d -> (o j) p t d", p=P, t=2)[bass.ds(j, 1)]
                sp.dma_start(xt[:, :, :], src.rearrange("o p t d -> (o p) t d")).then_inc(tail_loaded, 16)

            def tail_store(tt, b, j):
                sp.wait_ge(tdve, ND * tt + DV["ob"])
                sp.wait_ge(raw_loaded, 1)
                dst = out[bass.ds(b, 1), :, :].rearrange("o (j t p) d -> (o j) p t d", p=P, t=2)[bass.ds(j, 1)]
                sp.dma_start(dst.rearrange("o p t d -> (o p) t d"), yt[:, :, :]).then_inc(out_stored, 16)

            def iteration(it, b, g, first=False, turn=False, tail=False):
                if not first:
                    recips(it - 1, QH - 1)
                dup(it, 0)
                dup(it, 1)
                max_to_row(it, 0)
                max_to_row(it, 1)
                if turn:
                    y_turn(b)
                nxt = it + 1
                for p in range(4):
                    load_piece(nxt, p, (nxt // NQ) % B, nxt % NQ)
                if started(4 * it):
                    sp.wait_ge(wo_mm, 4 * it)
                if not isinstance(it, int):
                    sp.wait_ge(raw_loaded, 1)
                sp.dma_start(WoS[:, :, :], wo[bass.ds(g, 1), :, :, :].rearrange("o r p d -> p (o r) d")).then_inc(wo_loaded, 16)
                if tail:
                    tail_load(it - NQ, b - 1, g)
                max_to_row(it, 2)
                sums(it, 0)
                recips(it, 0)
                max_to_row(it, 3)
                sums(it, 1)
                recips(it, 1)
                sums(it, 2)
                recips(it, 2)
                if tail:
                    tail_store(it - NQ, b - 1, g)
                sums(it, 3)

            sp.sem_inc(out_stored, 16)
            for p in range(4):
                load_piece(0, p, 0, 0)
            sp.dma_start(gm[:, :], gamma.partition_broadcast(P).rearrange("e o n -> e (o n)")).then_inc(consts_loaded, 16)
            sp.dma_start(bt[:, :], beta.partition_broadcast(P).rearrange("e o n -> e (o n)")).then_inc(consts_loaded, 16)
            sp.dma_start(HT[:, :, 0:HID].bitcast(I32), wg).then_inc(ffn_raw, 16)
            sp.wait_ge(ffn_w, 1)
            sp.dma_start(HT[:, :, 0:HID].bitcast(I32), wu).then_inc(ffn_raw, 16)
            sp.wait_ge(ffn_w, 2)
            sp.dma_start(HT[:, :, 0:HID].bitcast(I32), wd).then_inc(ffn_raw, 16)
            iteration(0, 0, 0, first=True, turn=True)
            with sp.Fori(1, NQ) as g:
                iteration(g, 0, g)
            with sp.Fori(1, B) as b:
                iteration(NQ * b, b, 0, turn=True, tail=True)
                with sp.Fori(1, NQ) as g:
                    iteration(NQ * b + g, b, g, tail=True)
            recips(NIT - 1, QH - 1)
            y_turn(B)
            with sp.Fori(0, NQ) as j:
                tail_load(NIT - NQ + j, B - 1, j)
                tail_store(NIT - NQ + j, B - 1, j)
            sp.wait_ge(out_stored, 16 * (NIT + 1))

        @block.tensor
        def _(pe):
            mm, tr = nc.tensor.matmul, nc.tensor.transpose

            def proj(it, pair, u):
                n = 8 * it + 4 * pair + u
                if pair == 0 and u < 2:
                    if started(NST * it):
                        pe.wait_ge(hi_done, NST * it)
                else:
                    pe.wait_ge(proj_lo, 2 * n - 2)
                c, kind = u % 2, u // 2
                col = kind * QH * E + pair * 2 * E
                terms = [(wh, xh), (wh, xl), (wl, xh)]
                for k in range(KD):
                    for t, (a, b) in enumerate(terms):
                        last = mm(misc[u % 2][:, :], a[:, k, col:col + 2 * E], b[:, k, CH * c:CH * c + CH],
                                  start=(k == 0 and t == 0), stop=(k == KD - 1 and t == 2))
                last.then_inc(proj_mm, 1)

            def v_unit(it, u):
                if u < 2:
                    pe.wait_ge(proj_lo, 16 * it + 14 + 2 * u)
                else:
                    pe.wait_ge(v_lo, 8 * it + 2 * u - 2)
                col = 2 * QH * E
                for t in range(2):
                    tok = P * (2 * u + t)
                    n = 0
                    for k in range(KD):
                        for a, b in ((xh, wh), (xl, wh), (xh, wl)):
                            last = mm(misc[u % 2][:, 2 * P * t:2 * P * t + 2 * P], a[:, k, tok:tok + P],
                                      b[:, k, col:col + QH * E], start=(n == 0), stop=(n == 3 * KD - 1))
                            n += 1
                last.then_inc(v_mm, 1)

            def wo_unit(wi, u):
                if u == 0:
                    pe.wait_ge(ht_norm, 2 * (wi + 1))
                    pe.wait_ge(wo_loaded, 16 * (wi + 1))
                if u >= 2:
                    pe.wait_ge(y_added, 4 * wi + u - 1)
                for t in range(2):
                    tok = P * (2 * u + t)
                    for r in range(2):
                        last = mm(misc[u % 2][:, D * t:D * t + D], HT[:, r, tok:tok + P], WoS[:, r, :],
                                  start=(r == 0), stop=(r == 1))
                last.then_inc(wo_mm, 1)

            def max_chunk(it, n, k):
                e = RING_AT["c", n, k]
                if started(NMX * it + e - 1):
                    pe.wait_ge(mx_read, NMX * it + e - 1)
                j, c = CHUNKS[k]
                width = min(CH, P * (j + 1) - CH * c)
                diag = P * j - CH * c
                masked = diag < CH
                last = mm(mxb[e % 2][:, 0:width], Q1[:, n, P * j:P * j + P], K1[:, n, CH * c:CH * c + width],
                          start=True, stop=not masked)
                if masked:
                    last = mm(mxb[e % 2][:, diag:diag + P], identb[:, :], maskS[:, :], start=False, stop=True)
                last.then_inc(mx_mm, 1)

            def max_transpose(it, n):
                e = RING_AT["t", n, 0]
                pe.wait_ge(mx_read, NMX * it + e - 1)
                pe.wait_ge(mx_comb, QH * it + n + 1)
                tr(mxb[e % 2][0:TT, 0:P], mp[:, n % 2, 0:TT], identf[:, :]).then_inc(mx_mm, 1)

            def scores(it, s):
                n, (i, c) = s // NS, STEPS[s % NS]
                if started(NST * it + s - 1):
                    pe.wait_ge(exp_done, NST * it + s - 1)
                if s % NS == 0:
                    pe.wait_ge(max_row[n], 16 * (it + 1))
                o, lo = step_cols(i, c)
                q0 = CH * c
                mm(stb[s % 2][:, o:CH], K1[:, n, P * i:P * i + P], Q1[:, n, q0 + o:q0 + CH], start=True, stop=False)
                masked = P * i >= q0
                last = mm(stb[s % 2][:, o:CH], K2[:, n, P * i:P * i + P], Q2[:, n, q0 + o:q0 + CH],
                          start=False, stop=not masked)
                if masked:
                    last = mm(stb[s % 2][:, o:lo + P], identb[:, :], maskT[:, P - (lo - o):2 * P],
                              start=False, stop=True)
                last.then_inc(st_mm, 1)

            def pv(it, s):
                n, (i, c) = s // NS, STEPS[s % NS]
                if i == 0:
                    if started(2 * QH * it + 2 * n + c - 1):
                        pe.wait_ge(ht_copied, 2 * QH * it + 2 * n + c - 1)
                pe.wait_ge(lo_done, NST * it + s + 1)
                o, _ = step_cols(i, c)
                v0 = 0 if n % 2 == 0 else E
                ops = [(VH, ph), (VH, pl), (VL, ph)]
                for t, (a, b) in enumerate(ops):
                    last = mm(pvb[c][:, o:CH], a[:, i, n // 2, v0:v0 + P], b[:, s % RING, o:CH],
                              start=(i == 0 and t == 0), stop=(i == 4 * c + 3 and t == 2))
                last.then_inc(pv_mm, 1)

            def t_transpose(tt):
                pe.wait_ge(tdve, ND * tt + DV["x1b"])
                pe.wait_ge(v_lo, 8 * (tt + NQ + 1))
                pe.wait_ge(y_added, 4 * (tt + NQ))
                for k in range(KD):
                    for t in range(2):
                        last = tr(misc[0][:, 2 * P * k + P * t:2 * P * k + P * t + P], yt[:, t, P * k:P * k + P], identf[:, :])
                last.then_inc(tpe, 1)

            def t_up(tt, r):
                if r == 0:
                    pe.wait_ge(ffn_w, 3)
                    pe.wait_ge(tdve, ND * tt + DV["x1lo"])
                else:
                    pe.wait_ge(tdve, ND * tt + DV[f"h{r - 1}"])
                for wt, bk in ((Wg, misc[0]), (Wu, misc[1])):
                    for q in range(2):
                        m = 2 * r + q
                        n = 0
                        for k in range(KD):
                            for xx in (x1h, x1l):
                                last = mm(bk[:, 2 * P * q:2 * P * q + 2 * P], wt[:, k, P * m:P * m + P], xx[:, k, :],
                                          start=(n == 0), stop=(n == 2 * KD - 1))
                                n += 1
                    last.then_inc(tpe, 1)

            def t_down(tt, r):
                pe.wait_ge(tpool, NP * tt + PL[f"hl{r}"])
                if r == 0:
                    pe.wait_ge(mx_read, NMX * (tt + NQ + 1))
                for t in range(2):
                    for q in range(2):
                        for z, hx in enumerate((hh, hl)):
                            last = mm(mxb[t][:, 0:D], hx[:, q, P * t:P * t + P], Wd[:, 2 * r + q, :],
                                      start=(r == 0 and q == 0 and z == 0), stop=(r == 2 and q == 1 and z == 1))
                last.then_inc(tpe, 1)

            def iteration(it, first=False, tail=False):
                pe.wait_ge(raw_split, 4 * (it + 1))
                for pair in range(2):
                    for u in range(4):
                        proj(it, pair, u)
                if first:
                    pe.wait_ge(const_b, 3)
                for u in range(4):
                    v_unit(it, u)
                    if u == 0:
                        pe.wait_ge(proj_lo, 16 * it + 8)
                        pe.wait_ge(qk_dup[0], 64 * (it + 1))
                    for k in range(3 * u, 3 * u + 3):
                        max_chunk(it, 0, k)
                if not first:
                    pe.wait_ge(v_lo, 8 * (it + 1))
                for u in range(4):
                    if not first:
                        wo_unit(it - 1, u)
                    for k in range(3 * u, 3 * u + 3):
                        max_chunk(it, 1, k)
                    if u == 1:
                        max_transpose(it, 0)
                max_transpose(it, 1)
                pe.wait_ge(proj_lo, 16 * (it + 1))
                pe.wait_ge(qk_dup[1], 64 * (it + 1))
                pe.wait_ge(v_lo, 8 * (it + 1))
                if first:
                    pe.wait_ge(buf_init, 14)
                for s in range(NST):
                    scores(it, s)
                    if s < 2 * NS:
                        max_chunk(it, 2 + s // NS, s % NS)
                    if s in MAXT_AT:
                        max_transpose(it, MAXT_AT[s])
                    if s >= LAG:
                        pv(it, s - LAG)
                    if tail:
                        if s == T_TR:
                            t_transpose(it - NQ)
                        if s in T_UP:
                            t_up(it - NQ, T_UP.index(s))
                        if s in T_DOWN:
                            t_down(it - NQ, T_DOWN.index(s))
                for s in range(NST - LAG, NST):
                    pv(it, s)

            iteration(0, first=True)
            with pe.Fori(1, NQ) as it:
                iteration(it)
            with pe.Fori(NQ, NIT) as it:
                iteration(it, tail=True)
            for u in range(4):
                if u == 0:
                    pe.wait_ge(tdve, ND * (NIT - NQ))
                wo_unit(NIT - 1, u)
            pe.wait_ge(y_added, 4 * NIT)
            with pe.Fori(NIT - NQ, NIT) as tt:
                pe.wait_ge(tdve, ND * tt + DV["x1b"])
                for k in range(KD):
                    for t in range(2):
                        last = tr(misc[0][:, 2 * P * k + P * t:2 * P * k + P * t + P], yt[:, t, P * k:P * k + P], identf[:, :])
                last.then_inc(tpe, 1)
                for r in range(3):
                    t_up(tt, r)
                    pe.wait_ge(tpool, NP * tt + PL[f"hl{r}"])
                    for t in range(2):
                        for q in range(2):
                            for z, hx in enumerate((hh, hl)):
                                last = mm(mxb[t][:, 0:D], hx[:, q, P * t:P * t + P], Wd[:, 2 * r + q, :],
                                          start=(r == 0 and q == 0 and z == 0), stop=(r == 2 and q == 1 and z == 1))
                    last.then_inc(tpe, 1)

        @block.scalar
        def _(act):
            A = nc.scalar.activation

            def stage(nxt, p):
                act.wait_ge(raw_loaded, 16 * (4 * nxt + p + 1))
                if p == 0:
                    if started(4 * nxt):
                        act.wait_ge(v_mm, 4 * nxt)
                if p < KD:
                    A(xh[:, p, :], raw[:, :], ACT.Copy).then_inc(raw_hi, 1)
                else:
                    A(wh[:, p - KD, :], raw[:, 0:WC], ACT.Copy).then_inc(raw_hi, 1)

            def proj_evac(it, pair, u):
                c, kind = u % 2, u // 2
                act.wait_ge(proj_mm, 8 * it + 4 * pair + u + 1)
                if u == 0 and not (isinstance(it, int) and it == 0):
                    act.wait_ge(st_mm, NST * (it - 1) + 2 * NS * (pair + 1))
                dst = (Q1, K1)[kind]
                sc = SCALE if kind == 0 else 1.0
                for hd, rows in ((0, slice(0, E)), (1, slice(E, P))):
                    A(dst[rows, 2 * pair + hd, CH * c:CH * c + CH], misc[u % 2][rows, :], ACT.Copy, scale=sc).then_inc(proj_hi, 1)

            def v_evac(it, u):
                act.wait_ge(v_mm, 4 * it + u + 1)
                if u == 0:
                    if started(NST * it):
                        act.wait_ge(pv_mm, NST * it)
                for t in range(2):
                    dst = VH[:, 2 * u + t, :, :].rearrange("p r (a e) -> p r a e", e=E)[:, :, 0:3:2, :]
                    src = misc[u % 2][:, 2 * P * t:2 * P * t + 2 * P].rearrange("p (r a e) -> p r a e", r=2, a=2)
                    A(dst, src, ACT.Copy).then_inc(v_hi, 1)

            def exp(it, s):
                i, c = STEPS[s % NS]
                o, _ = step_cols(i, c)
                act.wait_ge(st_mm, NST * it + s + 1)
                if started(NST * it + s - 1):
                    act.wait_ge(lo_done, NST * it + s - 1)
                A(pe_[:, s % 2, o:CH], stb[s % 2][:, o:CH], ACT.Exp).then_inc(exp_done, 1)

            def copy_out(it, n, c):
                act.wait_ge(pv_mm, NST * it + NS * n + (4 if c == 0 else NS))
                if n < 2 and c == 0:
                    if started(4 * it):
                        act.wait_ge(wo_mm, 4 * it)
                if c == 0:
                    if started(16 * (QH * it + n - 1)):
                        act.wait_ge(sums_loaded, 16 * (QH * it + n - 1))
                rows, srow = (slice(0, E), E) if n % 2 == 0 else (slice(E, P), 0)
                cols = slice(CH * c, CH * c + CH)
                A(HT[rows, n // 2, cols], pvb[c][rows, :], ACT.Copy)
                A(rsum[srow:srow + 1, cols], pvb[c][srow:srow + 1, :], ACT.Copy).then_inc(ht_copied, 1)

            def t_x1(tt):
                act.wait_ge(tpe, NPE * tt + PEC["tr"])
                A(x1h[:, :, :], misc[0][:, :].rearrange("p (k n) -> p k n", k=KD), ACT.Copy).then_inc(tact, 1)

            def t_tanh(tt, r):
                act.wait_ge(tpe, NPE * tt + PEC[f"u{r}"])
                if r:
                    act.wait_ge(tpool, NP * tt + PL[f"hl{r - 1}"])
                A(th[:, :, :], misc[0][:, :].rearrange("p (k n) -> p k n", k=2), ACT.Tanh, scale=0.5 * WSCALE).then_inc(tact, 1)

            def t_hh(tt, r):
                act.wait_ge(tdve, ND * tt + DV[f"h{r}"])
                if r:
                    act.wait_ge(tpe, NPE * tt + PEC[f"d{r - 1}"])
                A(hh[:, :, :], th[:, :, :], ACT.Copy).then_inc(tact, 1)

            def iteration(it, tail=False):
                for pair in range(2):
                    for u in range(4):
                        proj_evac(it, pair, u)
                for u in range(4):
                    v_evac(it, u)
                for s in range(NST):
                    exp(it, s)
                    if s in COPY_AT:
                        copy_out(it, *COPY_AT[s])
                    if s in STAGE_AT:
                        stage(it + 1, STAGE_AT.index(s))
                    if tail:
                        if s == T_X1S:
                            t_x1(it - NQ)
                        if s in T_GATE:
                            t_tanh(it - NQ, T_GATE.index(s))
                        if s in T_HS:
                            t_hh(it - NQ, T_HS.index(s))
                copy_out(it, QH - 1, 1)

            for p in range(4):
                stage(0, p)
            iteration(0)
            with act.Fori(1, NQ) as it:
                iteration(it)
            with act.Fori(NQ, NIT) as it:
                iteration(it, tail=True)
            with act.Fori(NIT - NQ, NIT) as tt:
                t_x1(tt)
                for r in range(3):
                    t_tanh(tt, r)
                    t_hh(tt, r)

        @block.vector
        def _(dve):
            V = nc.vector

            def proj_rest(it, pair, u):
                c, kind = u % 2, u // 2
                n = 16 * it + 8 * pair + 2 * u
                cols = slice(CH * c, CH * c + CH)
                for hd, rows in ((0, slice(0, E)), (1, slice(E, P))):
                    hx = 2 * pair + hd
                    dve.wait_ge(proj_hi, n + hd + 1)
                    if kind == 0:
                        V.scalar_tensor_tensor(Q2[rows, hx, cols], misc[u % 2][rows, :], SCALE,
                                               Q1[rows, hx, cols].bitcast(F32), ALU.mult, ALU.subtract).then_inc(proj_lo, 1)
                    else:
                        other = slice(E, P) if hd == 0 else slice(0, E)
                        V.tensor_tensor(K1[other, hx, cols], misc[u % 2][rows, :],
                                        K1[rows, hx, cols].bitcast(F32), ALU.subtract).then_inc(proj_lo, 1)

            def v_rest(it, u):
                dve.wait_ge(v_hi, 8 * it + 2 * u + 2)
                for t in range(2):
                    def part(X):
                        return X[:, 2 * u + t, :, :].rearrange("p r (a e) -> p r a e", e=E)[:, :, 0:3:2, :]
                    src = misc[u % 2][:, 2 * P * t:2 * P * t + 2 * P].rearrange("p (r a e) -> p r a e", r=2, a=2)
                    V.tensor_tensor(part(VL), src, part(VH).bitcast(F32), ALU.subtract).then_inc(v_lo, 1)

            def max_chunk(it, n, k):
                e = RING_AT["c", n, k]
                dve.wait_ge(mx_mm, NMX * it + e + 1)
                if k == 0:
                    if started(NMX * it + (RING_AT["t", n - 2, 0] + 1 if n >= 2 else 0)):
                        dve.wait_ge(mx_mm, NMX * it + (RING_AT["t", n - 2, 0] + 1 if n >= 2 else 0))
                j, c = CHUNKS[k]
                width = min(CH, P * (j + 1) - CH * c)
                at = j if c == 0 else TT + j - 4
                V.reduce_max(mp[:, n % 2, at:at + 1], mxb[e % 2][:, 0:width], AX.X).then_inc(mx_read, 1)
                if k == NC - 1:
                    dve.wait_ge(mx_read, NMX * it + e + 1)
                    V.tensor_tensor(mp[:, n % 2, 4:TT], mp[:, n % 2, 4:TT], mp[:, n % 2, TT:NC], ALU.max).then_inc(mx_comb, 1)

            def max_row8(it, n):
                e = RING_AT["t", n, 0]
                dve.wait_ge(mx_mm, NMX * it + e + 1)
                if n >= 2:
                    dve.wait_ge(max_row[n - 2], 16 * (it + 1))
                else:
                    if started(16 * it):
                        dve.wait_ge(max_row[n + 2], 16 * it)
                V.tensor_scalar(M8[:, n % 2, :], mxb[e % 2][0:TT, 0:P], -1.0, None, ALU.mult).then_inc(mx_read, 1)

            def probs_hi(it, s):
                i, c = STEPS[s % NS]
                o, _ = step_cols(i, c)
                dve.wait_ge(exp_done, NST * it + s + 1)
                if started(NST * it + s - RING + 1):
                    dve.wait_ge(pv_mm, NST * it + s - RING + 1)
                V.tensor_copy(ph[:, s % RING, o:CH], pe_[:, s % 2, o:CH]).then_inc(hi_done, 1)

            def recip(it, n):
                k = QH * it + n
                dve.wait_ge(sums_loaded, 16 * (k + 1))
                if started(16 * k):
                    dve.wait_ge(recip_stored, 16 * k)
                if started(2 * it + n // 2):
                    dve.wait_ge(ht_norm, 2 * it + n // 2)
                V.reciprocal(R64[:, :], S64[:, :]).then_inc(recip_done, 1)

            def y_add(wi, u, seq):
                dve.wait_ge(wo_mm, 4 * wi + u + 1)
                if u == 0:
                    dve.wait_ge(y_inited, 16 * (seq + 1))
                yy = y[:, 2 * u:2 * u + 2, :]
                V.tensor_tensor(yy, misc[u % 2][:, :].rearrange("p (t d) -> p t d", t=2), yy, ALU.add).then_inc(y_added, 1)

            def own(tt, key):
                dve.wait_ge(tdve, ND * tt + DV[key])

            def stats(tt, x2, keys):
                for t in range(2):
                    V.bn_stats(st[:, t, :], x2[:, t, :]).then_inc(tdve, 1)
                own(tt, keys[1])
                V.memset(carrier[:, :], 0.0)
                for t in range(2):
                    V.bn_aggr(mv[:, t, :], st[:, t, :]).then_inc(tdve, 1)

            def normalise(tt, x2, key):
                dve.wait_ge(tpool, NP * tt + PL[key])
                for t in range(2):
                    V.tensor_scalar(x2[:, t, :], x2[:, t, :], mv[:, t, 0:1], rs[:, t:t + 1], ALU.subtract, ALU.mult).then_inc(tdve, 1)

            def t_ln1(tt):
                dve.wait_ge(tail_loaded, 32 * (tt + 1))
                stats(tt, yt, ["st1a", "st1b"])

            def t_add(tt):
                dve.wait_ge(tpool, NP * tt + PL["gam"])
                V.tensor_tensor(yt[:, :, :], yt[:, :, :], xt[:, :, :], ALU.add).then_inc(tdve, 1)
                own(tt, "add")
                stats(tt, yt, ["st2a", "st2b"])

            def t_x1lo(tt):
                dve.wait_ge(tact, NA * tt + AC["x1hi"])
                V.tensor_tensor(x1l[:, :, :], misc[0][:, :].rearrange("p (k n) -> p k n", k=KD),
                                x1h[:, :, :].bitcast(F32), ALU.subtract).then_inc(tdve, 1)

            def t_glu(tt, r):
                dve.wait_ge(tact, NA * tt + AC[f"tanh{r}"])
                V.scalar_tensor_tensor(th[:, :, :], th[:, :, :], 1.0, misc[0][:, :].rearrange("p (k n) -> p k n", k=2),
                                       ALU.add, ALU.mult).then_inc(tdve, 1)
                own(tt, f"tg{r}")
                V.tensor_tensor(th[:, :, :], misc[1][:, :].rearrange("p (k n) -> p k n", k=2), th[:, :, :], ALU.mult).then_inc(tdve, 1)

            def t_y2(tt):
                dve.wait_ge(tpe, NPE * tt + PEC["d2"])
                for t in range(2):
                    V.scalar_tensor_tensor(yt[:, t, :], mxb[t][:, 0:D], 0.5 * WSCALE ** 3, yt[:, t, :],
                                           ALU.mult, ALU.add).then_inc(tdve, 1)
                own(tt, "y2b")
                stats(tt, yt, ["st3a", "st3b"])

            def iteration(it, first=False, tail=False):
                if not first:
                    recip(it - 1, QH - 1)
                for pair in range(2):
                    for u in range(4):
                        proj_rest(it, pair, u)
                for u in range(4):
                    v_rest(it, u)
                    for k in range(3 * u, 3 * u + 3):
                        max_chunk(it, 0, k)
                for u in range(4):
                    if not first:
                        y_add(it - 1, u, (it - 1) // NQ)
                    for k in range(3 * u, 3 * u + 3):
                        max_chunk(it, 1, k)
                    if u == 1:
                        max_row8(it, 0)
                max_row8(it, 1)
                for s in range(NST):
                    probs_hi(it, s)
                    if s < 2 * NS:
                        max_chunk(it, 2 + s // NS, s % NS)
                    if s in MAXT_AT:
                        max_row8(it, MAXT_AT[s])
                    if s in RECIP_AT:
                        recip(it, RECIP_AT[s])
                    if tail:
                        tt = it - NQ
                        if s == T_LN1:
                            t_ln1(tt)
                        if s == T_LN1N:
                            normalise(tt, yt, "r1")
                        if s == T_ADD:
                            t_add(tt)
                        if s == T_X1:
                            normalise(tt, yt, "r2")
                        if s == T_X1S:
                            t_x1lo(tt)
                        if s in T_GATE:
                            t_glu(tt, T_GATE.index(s))
                        if s == T_Y2:
                            t_y2(tt)
                        if s == T_OUT:
                            normalise(tt, yt, "r3")

            V.memset(VH[:, :, :, E:2 * E].bitcast(F32), 1.0).then_inc(buf_init, 1)
            V.memset(VL[:, :, :, E:2 * E].bitcast(F32), 0.0).then_inc(buf_init, 1)
            for pair in range(2):
                a, b = 2 * pair, 2 * pair + 1
                for X in (Q2, K2):
                    V.memset(X[E:P, a, :].bitcast(F32), 0.0).then_inc(buf_init, 1)
                    V.memset(X[0:E, b, :].bitcast(F32), 0.0).then_inc(buf_init, 1)
            dve.wait_ge(buf_init, 10)
            for pair in range(2):
                V.memset(K2[E:E + 1, 2 * pair, :].bitcast(F32), 1.0).then_inc(buf_init, 1)
                V.memset(K2[0:1, 2 * pair + 1, :].bitcast(F32), 1.0).then_inc(buf_init, 1)
            dve.wait_ge(const_step, 8)
            V.tensor_copy(maskT[:, :], mraw[:, 0:2 * P]).then_inc(const_b, 1)
            V.tensor_copy(maskS[:, :], mraw[:, 2 * P:3 * P]).then_inc(const_b, 1)
            V.tensor_copy(identb[:, :], identf[:, :]).then_inc(const_b, 1)
            iteration(0, first=True)
            with dve.Fori(1, NQ) as it:
                iteration(it)
            with dve.Fori(NQ, NIT) as it:
                iteration(it, tail=True)
            recip(NIT - 1, QH - 1)
            for u in range(4):
                y_add(NIT - 1, u, B - 1)
            with dve.Fori(NIT - NQ, NIT) as tt:
                t_ln1(tt)
                normalise(tt, yt, "r1")
                t_add(tt)
                normalise(tt, yt, "r2")
                t_x1lo(tt)
                for r in range(3):
                    t_glu(tt, r)
                t_y2(tt)
                normalise(tt, yt, "r3")

        @block.gpsimd
        def _(pool):
            G = nc.gpsimd

            def stage(nxt, p):
                pool.wait_ge(raw_hi, 4 * nxt + p + 1)
                if p < KD:
                    G.tensor_tensor(xl[:, p, :], raw[:, :], xh[:, p, :].bitcast(F32), ALU.subtract).then_inc(raw_split, 1)
                else:
                    G.tensor_tensor(wl[:, p - KD, :], raw[:, 0:WC], wh[:, p - KD, :].bitcast(F32), ALU.subtract).then_inc(raw_split, 1)

            def probs_lo(it, s):
                i, c = STEPS[s % NS]
                o, _ = step_cols(i, c)
                pool.wait_ge(hi_done, NST * it + s + 1)
                G.tensor_tensor(pl[:, s % RING, o:CH], pe_[:, s % 2, o:CH], ph[:, s % RING, o:CH].bitcast(F32),
                                ALU.subtract).then_inc(lo_done, 1)

            def norm(it, pair):
                pool.wait_ge(recip_bc, 16 * (QH * it + 2 * pair + 2))
                G.tensor_tensor(HT[:, pair, :], HT[:, pair, :], RB[:, :], ALU.mult).then_inc(ht_norm, 1)

            def own(tt, key):
                pool.wait_ge(tpool, NP * tt + PL[key])

            def rstd(tt, eps, dkey, ekey):
                pool.wait_ge(tdve, ND * tt + DV[dkey])
                G.tensor_tensor(rs[:, :], mv[:, :, 1:2].rearrange("p t o -> p (t o)"), eps[:, :], ALU.add).then_inc(tpool, 1)
                own(tt, ekey)
                G.tensor_tensor(rs[:, :], rs[:, :], halves[:, :], ALU.pow).then_inc(tpool, 1)

            def t_xb(tt):
                pool.wait_ge(tail_loaded, 32 * (tt + 1))
                pool.wait_ge(consts_loaded, 32)
                G.tensor_tensor(xt[:, :, :], xt[:, :, :], bt[:, :].rearrange("p (o d) -> p o d", o=1).broadcast_to([P, 2, D]), ALU.add).then_inc(tpool, 1)

            def t_gamma(tt):
                pool.wait_ge(tdve, ND * tt + DV["n1b"])
                G.tensor_tensor(yt[:, :, :], yt[:, :, :], gm[:, :].rearrange("p (o d) -> p o d", o=1).broadcast_to([P, 2, D]), ALU.mult).then_inc(tpool, 1)

            def t_hl(tt, r):
                pool.wait_ge(tact, NA * tt + AC[f"hh{r}"])
                G.tensor_tensor(hl[:, :, :], th[:, :, :], hh[:, :, :].bitcast(F32), ALU.subtract).then_inc(tpool, 1)

            def iteration(it, first=False, tail=False):
                if not first:
                    norm(it - 1, 1)
                for s in range(NST):
                    probs_lo(it, s)
                    if s in STAGE_AT:
                        stage(it + 1, STAGE_AT.index(s))
                    if s in NORM_AT:
                        norm(it, NORM_AT[s])
                    if tail:
                        tt = it - NQ
                        if s == T_LN1:
                            t_xb(tt)
                        if s == T_LN1R:
                            rstd(tt, eps_attn, "mv1b", "e1")
                        if s == T_AFF:
                            t_gamma(tt)
                        if s == T_LN2R:
                            rstd(tt, eps_ln, "mv2b", "e2")
                        if s in T_HL:
                            t_hl(tt, T_HL.index(s))
                        if s == T_LN3R:
                            rstd(tt, eps_ln, "mv3b", "e3")

            G.memset(identf[:, :], 0.0).then_inc(const_step, 1)
            G.memset(mraw[:, :], 0.0).then_inc(const_step, 1)
            G.memset(halves[:, :], -0.5).then_inc(const_step, 1)
            G.memset(eps_attn[:, :], LN_EPS_ATTN).then_inc(const_step, 1)
            G.memset(eps_ln[:, :], LN_EPS).then_inc(const_step, 1)
            pool.wait_ge(const_step, 5)
            G.affine_select(out=identf[:, :], in_=identf[:, :], compare_op=ALU.not_equal, fill=1.0, base=0,
                            pattern=[[-1, P]], channel_multiplier=1).then_inc(const_step, 1)
            G.affine_select(out=mraw[:, 0:2 * P], in_=mraw[:, 0:2 * P], compare_op=ALU.is_ge, fill=MASKED, base=-P,
                            pattern=[[1, 2 * P]], channel_multiplier=-1).then_inc(const_step, 1)
            G.affine_select(out=mraw[:, 2 * P:3 * P], in_=mraw[:, 2 * P:3 * P], compare_op=ALU.is_ge, fill=MASKED, base=0,
                            pattern=[[-1, P]], channel_multiplier=1).then_inc(const_step, 1)
            for p in range(4):
                stage(0, p)
            for n, wt in enumerate((Wg, Wu, Wd)):
                pool.wait_ge(ffn_raw, 16 * (n + 1))
                dst = wt[:, :, :] if n < 2 else wt[:, :, :].rearrange("p (a b) d -> p a (b d)", a=2)
                G.tensor_copy(dst, HT[:, :, 0:HID].bitcast(I32)).then_inc(ffn_w, 1)
            iteration(0, first=True)
            with pool.Fori(1, NQ) as it:
                iteration(it)
            with pool.Fori(NQ, NIT) as it:
                iteration(it, tail=True)
            norm(NIT - 1, 1)
            with pool.Fori(NIT - NQ, NIT) as tt:
                t_xb(tt)
                rstd(tt, eps_attn, "mv1b", "e1")
                t_gamma(tt)
                rstd(tt, eps_ln, "mv2b", "e2")
                for r in range(3):
                    t_hl(tt, r)
                rstd(tt, eps_ln, "mv3b", "e3")


def kernel(L0_attn_x, L0_attn_Wq, L0_attn_Wk, L0_attn_Wv, L0_attn_Wo, L0_attn_gamma, L0_attn_beta,
           L0_ffn_w_gate, L0_ffn_w_up, L0_ffn_w_down):
    import numpy as np
    import concourse.bacc as bacc
    from concourse.bass_utils import run_bass_kernel_spmd as run

    x = np.ascontiguousarray(L0_attn_x)
    w3 = np.stack([np.asarray(a) for a in (L0_attn_Wq, L0_attn_Wk, L0_attn_Wv)])
    w3 = w3.reshape(3, NQ, QH, KD, P, E).transpose(1, 3, 4, 0, 2, 5).reshape(NQ, KD, P, 3 * QH * E)
    arrays = {
        "xT": x.transpose(0, 2, 1).reshape(B, KD, P, S),
        "x": x,
        "wqkv": w3,
        "wo": np.asarray(L0_attn_Wo).reshape(NQ, 2, P, D),
        "w_gate_T": np.asarray(L0_ffn_w_gate).T.reshape(KD, P, HID).transpose(1, 0, 2),
        "w_up_T": np.asarray(L0_ffn_w_up).T.reshape(KD, P, HID).transpose(1, 0, 2),
        "w_down_T": np.asarray(L0_ffn_w_down).T.reshape(NH6, P, D).transpose(1, 0, 2).reshape(P, 2, HID),
        "gamma": np.asarray(L0_attn_gamma).reshape(1, D),
        "beta": np.asarray(L0_attn_beta).reshape(1, D),
    }
    arrays = {k: np.ascontiguousarray(a) for k, a in arrays.items()}
    nc = bacc.Bacc("TRN2", target_bir_lowering=False, num_devices=1)
    aps = {k: nc.dram_tensor(k, a.shape, mybir.dt.from_np(a.dtype), kind="ExternalInput").ap() for k, a in arrays.items()}
    out = nc.dram_tensor("out", (B, S, D), F32, kind="ExternalOutput").ap()
    yscr = nc.dram_tensor("y_scratch", (S, D), F32, kind="Internal").ap()
    rscr = nc.dram_tensor("recip_scratch", (QH, S), F32, kind="Internal").ap()
    build(nc, aps["xT"], aps["x"], aps["wqkv"], aps["wo"], aps["w_gate_T"], aps["w_up_T"], aps["w_down_T"],
          aps["gamma"], aps["beta"], out, yscr, rscr)
    r = run(nc, [arrays], core_ids=[0])
    return r.results[0]["out"]
```

```python
import concourse.bass as bass
from concourse import mybir
from contextlib import ExitStack

F32 = mybir.dt.float32
F32R = mybir.dt.float32r
BF16 = mybir.dt.bfloat16
I32 = mybir.dt.int32
ALU = mybir.AluOpType
ACT = mybir.ActivationFunctionType
AX = mybir.AxisListType

P = 128
B, S, D = 4, 1024, 256
H, E = 16, 64
HID = 768
KD = D // P
QH = 4
NQ = H // QH
NIT = B * NQ
TT = S // P
CH = 512
NH6 = HID // P
LN_EPS_ATTN = 1e-3
LN_EPS = 1e-5
SCALE = float(E) ** -0.5
WSCALE = 1.0 / 127.0
MASKED = -1e30

STEPS = [(i, c) for c in range(S // CH) for i in range(4 * (c + 1))]
NS = len(STEPS)
NST = QH * NS
CHUNKS = [(j, c) for j in range(TT) for c in range(j // 4 + 1)]
NC = len(CHUNKS)
NMX = QH * (NC + 1)
LAG = 3
RING = 3


def step_cols(i, c):
    lo = max(0, P * i - CH * c)
    return min(lo, CH - 2 * P), lo


RING_ORDER = ([("c", 0, k) for k in range(NC)] + [("t", 0, 0)] + [("c", 1, k) for k in range(NC)] + [("t", 1, 0)]
              + [("c", 2, k) for k in range(NC)] + [("c", 3, k) for k in range(2)] + [("t", 2, 0)]
              + [("c", 3, k) for k in range(2, NC)] + [("t", 3, 0)])
RING_AT = {e: n for n, e in enumerate(RING_ORDER)}

MAX_AT = {s: (2 + s // NS, s % NS) for s in range(2 * NS)}
MAX_NEXT_AT = {35 + k: k for k in range(NC)}
MAXT_AT = {13: 2, 25: 3}
MAXT_NEXT_AT = 47
WO_AT = [1, 3, 4, 6]
PROJ_AT = [26, 28, 30, 32]
STAGE_AT = [3, 9, 15, 21]
COPY_AT = {12 * n + 7: (n, 0) for n in range(QH)} | {12 * n + 15: (n, 1) for n in range(QH - 1)}
RECIP_AT = {12 * n + 20: n for n in range(QH - 1)}
NORM_AT = 40
T_LN1, T_LN1R, T_LN1N, T_AFF, T_ADD, T_LN2R, T_X1 = 0, 1, 2, 4, 5, 6, 8
T_TR, T_X1S = 12, 13
T_UP, T_GATE, T_HS, T_HL, T_DOWN, T_Y2 = [14, 20, 34], [15, 21, 35], [16, 22, 36], [16, 22, 36], [18, 24, 38], [19, 25, 39]
T_LN3, T_LN3R, T_OUT = 40, 41, 42
TAIL_LAG = NQ + 1
LO_VECTOR = 3


def build(nc, xT, x, wqkv, wo, wg, wu, wd, gamma, beta, out, yscr, rscr):
    ctx = ExitStack()
    with ctx:
        def sb(name, shape, dt=F32):
            return ctx.enter_context(nc.sbuf_tensor(name, shape, dt))

        def sem(name):
            return ctx.enter_context(nc.semaphore(name))

        raw = sb("raw", [P, S])
        xh, xl = sb("xh", [P, KD, S], F32R), sb("xl", [P, KD, S], F32R)
        WC = 3 * QH * E
        wh, wl = sb("wh", [P, KD, WC], F32R), sb("wl", [P, KD, WC], F32R)
        Q1, Q2 = sb("Q1", [P, QH, S], F32R), sb("Q2", [P, QH, S], F32R)
        K1, K2 = sb("K1", [P, QH, S], F32R), sb("K2", [P, QH, S], F32R)
        VW = 3 * E
        VH, VL = sb("VH", [P, TT, 2, VW], F32R), sb("VL", [P, TT, 2, VW], F32R)
        pe_ = sb("probs", [P, 2, CH])
        ph, pl = sb("probs_hi", [P, RING, CH], F32R), sb("probs_lo", [P, RING, CH], F32R)
        HT = sb("heads_T", [P, 2, S])
        rsum = sb("row_sums", [P, S])
        RB = sb("recip_bc", [P, S])
        S64, R64 = sb("sums64", [E, S // E]), sb("recip64", [E, S // E])
        mp = sb("max_part", [P, 2, NC])
        M8 = sb("neg_max8", [TT, 2, P], F32R)
        WoS = sb("wo_quad", [P, 2, D])
        y = sb("y", [P, TT, D])
        Wg, Wu, Wd = sb("w_gate", [P, KD, HID], F32R), sb("w_up", [P, KD, HID], F32R), sb("w_down", [P, NH6, D], F32R)
        yt, xt = sb("y_tail", [P, 2, D]), sb("x_tail", [P, 2, D])
        x1h, x1l = sb("x1T_hi", [P, KD, 2 * P], F32R), sb("x1T_lo", [P, KD, 2 * P], F32R)
        th, hh, hl = sb("tanh_h", [P, 2, 2 * P]), sb("h_hi", [P, 2, 2 * P], F32R), sb("h_lo", [P, 2, 2 * P], F32R)
        gm, bt = sb("gamma_bc", [P, D]), sb("beta_bc", [P, D])
        st, mv, rs = sb("bn_st", [P, 2, 6]), sb("mean_var", [P, 2, 2]), sb("rstd", [P, 2])
        halves, eps_attn, eps_ln = sb("minus_half", [P, 2]), sb("eps_attn", [P, 2]), sb("eps_ln", [P, 2])
        carrier = sb("carrier", [1, 1])
        identf, identb = sb("ident_f", [P, P]), sb("ident_b", [P, P], BF16)
        maskS = sb("mask_keys_free", [P, P], BF16)
        maskT = sb("mask_queries_free", [P, 2 * P], BF16)
        mraw = th[:, :, :].rearrange("p a b -> p (a b)")

        bank = [ctx.enter_context(nc.psum_tensor(f"bank{i}", [P, CH], F32)) for i in range(8)]
        misc, mxb, stb, pvb = bank[0:2], bank[2:4], bank[4:6], bank[6:8]

        raw_loaded = sem("raw_loaded")
        qk_dup = [sem("qk_dup0"), sem("qk_dup1")]
        max_row = [sem(f"max_row{n}") for n in range(QH)]
        sums_loaded, recip_stored, recip_bc = sem("sums_loaded"), sem("recip_stored"), sem("recip_bc_loaded")
        wo_loaded, y_stored, y_inited = sem("wo_loaded"), sem("y_stored"), sem("y_inited")
        tail_loaded, out_stored = sem("tail_loaded"), sem("out_stored")
        ffn_raw, consts_loaded = sem("ffn_raw_loaded"), sem("consts_loaded")
        const_step, const_b = sem("const_step"), sem("const_bf16")
        buf_init = sem("buffers_initialised")
        ffn_w = sem("ffn_weights_ready")
        raw_hi, raw_split = sem("raw_hi_done"), sem("raw_split_done")
        proj_mm, proj_hi, proj_lo = sem("proj_mm"), sem("proj_hi"), sem("proj_lo")
        v_mm, v_hi, v_lo = sem("v_mm"), sem("v_hi"), sem("v_lo")
        mx_mm, mx_read, mx_comb = sem("max_scores"), sem("max_read"), sem("max_combined")
        st_mm, exp_done, hi_done, pv_mm = sem("scores_mm"), sem("exp_done"), sem("probs_hi_done"), sem("pv_mm")
        lo_dve, lo_pool = sem("probs_lo_vector"), sem("probs_lo_pool")
        ht_copied, recip_done, ht_norm = sem("heads_copied"), sem("recip_done"), sem("heads_normed")
        wo_mm, y_added = sem("wo_mm"), sem("y_added")
        tdve, tpool, tact, tpe = sem("tail_dve"), sem("tail_pool"), sem("tail_act"), sem("tail_pe")

        def started(v):
            assert isinstance(v, int) or v.min_val > 0, "a register's value has to be positive"
            return not isinstance(v, int) or v > 0

        DV = {k: n + 1 for n, k in enumerate(
            ["st1a", "st1b", "mv1a", "mv1b", "n1a", "n1b", "add", "st2a", "st2b", "mv2a", "mv2b", "x1a", "x1b", "x1lo"]
            + [f"{k}{r}" for r in range(3) for k in ("tg", "h", "y2")]
            + ["st3a", "st3b", "mv3a", "mv3b", "oa", "ob"])}
        PL = {k: n + 1 for n, k in enumerate(
            ["xb", "e1", "r1", "gam", "e2", "r2", "hl0", "hl1", "hl2", "e3", "r3"])}
        AC = {k: n + 1 for n, k in enumerate(["x1hi", "tanh0", "hh0", "tanh1", "hh1", "tanh2", "hh2"])}
        PEC = {k: n + 1 for n, k in enumerate(["tr", "g0", "u0", "d0", "g1", "u1", "d1", "g2", "u2", "d2"])}
        ND, NP, NA, NPE = len(DV), len(PL), len(AC), len(PEC)

        def lo_of(it, s):
            if s < 0:
                it, s = it - 1, s + NST
            if s % LO_VECTOR == LO_VECTOR - 1:
                return lo_dve, NST // LO_VECTOR * it + s // LO_VECTOR + 1
            return lo_pool, (NST - NST // LO_VECTOR) * it + s - s // LO_VECTOR + 1

        block = ctx.enter_context(nc.Block())

        @block.sync
        def _(sp):
            def bits(ap):
                return ap.bitcast(F32)

            def load_piece(nxt, p, seq_b, quad):
                if started(4 * nxt + p):
                    sp.wait_ge(raw_split, 4 * nxt + p)
                if not isinstance(nxt, int):
                    sp.wait_ge(raw_loaded, 1)
                if p < KD:
                    src = xT[bass.ds(seq_b, 1), p, :, :].rearrange("o p n -> (o p) n")
                    sp.dma_start(raw[:, :], src).then_inc(raw_loaded, 16)
                else:
                    src = wqkv[bass.ds(quad, 1), p - KD, :, :].rearrange("o p n -> (o p) n")
                    sp.dma_start(raw[:, 0:WC], src).then_inc(raw_loaded, 16)

            def dup(it, pair):
                a, b = 2 * pair, 2 * pair + 1
                sp.wait_ge(proj_hi, 16 * it + 8 * pair + 4)
                sp.dma_start(bits(Q1[E:P, a, :]), bits(Q1[0:E, a, :])).then_inc(qk_dup[pair], 16)
                sp.dma_start(bits(Q1[0:E, b, :]), bits(Q1[E:P, b, :])).then_inc(qk_dup[pair], 16)
                sp.wait_ge(proj_hi, 16 * it + 8 * pair + 8)
                sp.dma_start(bits(K2[0:E, a, :]), bits(K1[0:E, a, :])).then_inc(qk_dup[pair], 16)
                sp.dma_start(bits(K2[E:P, b, :]), bits(K1[E:P, b, :])).then_inc(qk_dup[pair], 16)

            def max_to_row(it, n):
                if isinstance(it, int) and it == 0:
                    sp.wait_ge(buf_init, 14)
                sp.wait_ge(mx_read, NMX * it + RING_AT["t", n, 0] + 1)
                row = E if n % 2 == 0 else 0
                sp.dma_start(bits(Q2[row:row + 1, n, :]).rearrange("o (j q) -> o j q", j=TT), bits(M8[:, n % 2, :]))\
                    .then_inc(max_row[n], 16)

            def sums(it, n):
                sp.wait_ge(ht_copied, 2 * QH * it + 2 * n + 2)
                row = E if n % 2 == 0 else 0
                sp.dma_start(S64[:, :], rsum[row:row + 1, :].rearrange("o (a b) -> o a b", a=E)).then_inc(sums_loaded, 16)

            def recips(it, n):
                k = QH * it + n
                sp.wait_ge(recip_done, k + 1)
                sp.dma_start(rscr[n:n + 1, :].rearrange("o (a b) -> (o a) b", a=E), R64[:, :]).then_inc(recip_stored, 16)
                sp.wait_ge(recip_stored, 16 * (k + 1))
                rows = slice(0, E) if n % 2 == 0 else slice(E, P)
                sp.dma_start(RB[rows, :], rscr[n:n + 1, :].partition_broadcast(E).rearrange("e o n -> e (o n)")
                             ).then_inc(recip_bc, 16)

            def y_turn(b):
                if not (isinstance(b, int) and b == 0):
                    sp.wait_ge(y_added, 16 * b)
                    sp.wait_ge(raw_loaded, 1)
                    sp.dma_start(yscr.rearrange("(t p) d -> p t d", p=P), y[:, :, :]).then_inc(y_stored, 16)
                    sp.wait_ge(y_stored, 16 * b)
                    sp.wait_ge(raw_loaded, 1)
                if not (isinstance(b, int) and b == B):
                    src = x[bass.ds(b, 1), :, :].rearrange("o (t p) d -> p (o t) d", p=P)
                    sp.dma_start(y[:, :, :], src).then_inc(y_inited, 16)

            def tail_load(tt):
                sp.wait_ge(out_stored, 16 * (tt + 1))
                sp.wait_ge(raw_loaded, 1)
                sp.dma_start(yt[:, :, :], yscr.rearrange("(j t p) d -> j p t d", p=P, t=2)[bass.ds(tt % NQ, 1)]
                             .rearrange("o p t d -> (o p) t d")).then_inc(tail_loaded, 16)
                src = x.rearrange("b (j t p) d -> (b j) p t d", p=P, t=2)[bass.ds(tt, 1)]
                sp.dma_start(xt[:, :, :], src.rearrange("o p t d -> (o p) t d")).then_inc(tail_loaded, 16)

            def tail_store(tt):
                sp.wait_ge(tdve, ND * tt + DV["ob"])
                sp.wait_ge(raw_loaded, 1)
                dst = out.rearrange("b (j t p) d -> (b j) p t d", p=P, t=2)[bass.ds(tt, 1)]
                sp.dma_start(dst.rearrange("o p t d -> (o p) t d"), yt[:, :, :]).then_inc(out_stored, 16)

            def iteration(it, first=False, turn=None, tail=False, last=False):
                nxt = it + 1
                if tail:
                    tail_load(it - TAIL_LAG)
                dup(it, 1)
                if not first:
                    sums(it - 1, QH - 1)
                    recips(it - 1, QH - 1)
                max_to_row(it, 1)
                if not last:
                    for p in range(3):
                        load_piece(nxt, p, nxt // NQ, nxt % NQ)
                if turn is not None:
                    if tail:
                        sp.wait_ge(tail_loaded, 32 * (it - TAIL_LAG + 1))
                    y_turn(turn)
                max_to_row(it, 2)
                sums(it, 0)
                if not last:
                    load_piece(nxt, 3, nxt // NQ, nxt % NQ)
                if not first:
                    sp.wait_ge(wo_mm, 4 * it)
                    sp.wait_ge(raw_loaded, 1)
                sp.dma_start(WoS[:, :, :], wo[bass.ds(it % NQ, 1), :, :, :].rearrange("o r p d -> p (o r) d")).then_inc(wo_loaded, 16)
                recips(it, 0)
                max_to_row(it, 3)
                sums(it, 1)
                if not last:
                    dup(nxt, 0)
                recips(it, 1)
                sums(it, 2)
                if tail:
                    tail_store(it - TAIL_LAG)
                recips(it, 2)
                if not last:
                    max_to_row(nxt, 0)

            sp.sem_inc(out_stored, 16)
            for p in range(4):
                load_piece(0, p, 0, 0)
            sp.dma_start(gm[:, :], gamma.partition_broadcast(P).rearrange("e o n -> e (o n)")).then_inc(consts_loaded, 16)
            sp.dma_start(bt[:, :], beta.partition_broadcast(P).rearrange("e o n -> e (o n)")).then_inc(consts_loaded, 16)
            sp.dma_start(HT[:, :, 0:HID].bitcast(I32), wg).then_inc(ffn_raw, 16)
            dup(0, 0)
            max_to_row(0, 0)
            sp.wait_ge(ffn_w, 1)
            sp.dma_start(HT[:, :, 0:HID].bitcast(I32), wu).then_inc(ffn_raw, 16)
            sp.wait_ge(ffn_w, 2)
            sp.dma_start(HT[:, :, 0:HID].bitcast(I32), wd).then_inc(ffn_raw, 16)
            iteration(0, first=True, turn=0)
            with sp.Fori(1, NQ) as it:
                iteration(it)
            for b in range(1, B):
                iteration(NQ * b, turn=b, tail=b > 1)
                with sp.Fori(NQ * b + 1, NQ * (b + 1) - (b == B - 1)) as it:
                    iteration(it, tail=True)
            iteration(NIT - 1, tail=True, last=True)
            sums(NIT - 1, QH - 1)
            recips(NIT - 1, QH - 1)
            tail_load(NIT - TAIL_LAG)
            sp.wait_ge(tail_loaded, 32 * (NIT - TAIL_LAG + 1))
            y_turn(B)
            tail_store(NIT - TAIL_LAG)
            with sp.Fori(NIT - NQ, NIT) as tt:
                tail_load(tt)
                tail_store(tt)
            sp.wait_ge(out_stored, 16 * (NIT + 1))

        @block.tensor
        def _(pe):
            mm, tr = nc.tensor.matmul, nc.tensor.transpose

            def proj(it, pair, u, first=False, y_at=0, tail=False):
                n = 8 * it + 4 * pair + u
                if pair == 0 and u == 0 and not first:
                    pe.wait_ge(v_lo, 8 * it)
                    if started(y_at):
                        pe.wait_ge(y_added, y_at)
                    if tail:
                        pe.wait_ge(tdve, ND * (it - 1 - TAIL_LAG) + DV["y21"])
                if pair == 0 and u == 0:
                    pe.wait_ge(raw_split, 4 * (it + 1))
                if u >= 2 or pair == 1:
                    pe.wait_ge(proj_lo, 2 * n - 2)
                if pair == 1 and u == 0 and started(NST // LO_VECTOR * it):
                    pe.wait_ge(lo_dve, NST // LO_VECTOR * it)
                c, kind = u % 2, u // 2
                col = kind * QH * E + pair * 2 * E
                terms = [(wh, xh), (wh, xl), (wl, xh)]
                for k in range(KD):
                    for t, (a, b) in enumerate(terms):
                        last = mm(misc[u % 2][:, :], a[:, k, col:col + 2 * E], b[:, k, CH * c:CH * c + CH],
                                  start=(k == 0 and t == 0), stop=(k == KD - 1 and t == 2))
                last.then_inc(proj_mm, 1)

            def v_unit(it, u):
                if u < 2:
                    pe.wait_ge(proj_lo, 16 * it + 14 + 2 * u)
                else:
                    pe.wait_ge(v_lo, 8 * it + 2 * u - 2)
                col = 2 * QH * E
                for t in range(2):
                    tok = P * (2 * u + t)
                    n = 0
                    for k in range(KD):
                        for a, b in ((xh, wh), (xl, wh), (xh, wl)):
                            last = mm(misc[u % 2][:, 2 * P * t:2 * P * t + 2 * P], a[:, k, tok:tok + P],
                                      b[:, k, col:col + QH * E], start=(n == 0), stop=(n == 3 * KD - 1))
                            n += 1
                last.then_inc(v_mm, 1)

            def wo_unit(wi, u, alone=False):
                if u == 0:
                    pe.wait_ge(ht_norm, 2 * (wi + 1))
                    pe.wait_ge(wo_loaded, 16 * (wi + 1))
                if u < 2 and not alone:
                    pe.wait_ge(v_lo, 8 * wi + 14 + 2 * u)
                if u >= 2:
                    pe.wait_ge(y_added, 4 * wi + u - 1)
                for t in range(2):
                    tok = P * (2 * u + t)
                    for r in range(2):
                        last = mm(misc[u % 2][:, D * t:D * t + D], HT[:, r, tok:tok + P], WoS[:, r, :],
                                  start=(r == 0), stop=(r == 1))
                last.then_inc(wo_mm, 1)

            def max_chunk(it, n, k):
                e = RING_AT["c", n, k]
                if started(NMX * it + e - 1):
                    pe.wait_ge(mx_read, NMX * it + e - 1)
                j, c = CHUNKS[k]
                width = min(CH, P * (j + 1) - CH * c)
                diag = P * j - CH * c
                masked = diag < CH
                last = mm(mxb[e % 2][:, 0:width], Q1[:, n, P * j:P * j + P], K1[:, n, CH * c:CH * c + width],
                          start=True, stop=not masked)
                if masked:
                    last = mm(mxb[e % 2][:, diag:diag + P], identb[:, :], maskS[:, :], start=False, stop=True)
                last.then_inc(mx_mm, 1)

            def max_transpose(it, n):
                e = RING_AT["t", n, 0]
                pe.wait_ge(mx_read, NMX * it + e - 1)
                pe.wait_ge(mx_comb, QH * it + n + 1)
                tr(mxb[e % 2][0:TT, 0:P], mp[:, n % 2, 0:TT], identf[:, :]).then_inc(mx_mm, 1)

            def scores(it, s):
                n, (i, c) = s // NS, STEPS[s % NS]
                if started(NST * it + s - 1):
                    pe.wait_ge(hi_done, NST * it + s - 1)
                if s % NS == 0:
                    pe.wait_ge(max_row[n], 16 * (it + 1))
                o, lo = step_cols(i, c)
                q0 = CH * c
                mm(stb[s % 2][:, o:CH], K1[:, n, P * i:P * i + P], Q1[:, n, q0 + o:q0 + CH], start=True, stop=False)
                masked = P * i >= q0
                last = mm(stb[s % 2][:, o:CH], K2[:, n, P * i:P * i + P], Q2[:, n, q0 + o:q0 + CH],
                          start=False, stop=not masked)
                if masked:
                    last = mm(stb[s % 2][:, o:lo + P], identb[:, :], maskT[:, P - (lo - o):2 * P],
                              start=False, stop=True)
                last.then_inc(st_mm, 1)

            def pv(it, s):
                n, (i, c) = s // NS, STEPS[s % NS]
                if i == 0:
                    if started(2 * QH * it + 2 * n + c - 1):
                        pe.wait_ge(ht_copied, 2 * QH * it + 2 * n + c - 1)
                pe.wait_ge(*lo_of(it, s))
                o, _ = step_cols(i, c)
                v0 = 0 if n % 2 == 0 else E
                ops = [(VH, ph), (VH, pl), (VL, ph)]
                for t, (a, b) in enumerate(ops):
                    last = mm(pvb[c][:, o:CH], a[:, i, n // 2, v0:v0 + P], b[:, s % RING, o:CH],
                              start=(i == 0 and t == 0), stop=(i == 4 * c + 3 and t == 2))
                last.then_inc(pv_mm, 1)

            def t_transpose(tt, alone=False):
                pe.wait_ge(tdve, ND * tt + DV["x1b"])
                if not alone:
                    pe.wait_ge(y_added, 4 * (tt + TAIL_LAG))
                for k in range(KD):
                    for t in range(2):
                        last = tr(misc[0][:, 2 * P * k + P * t:2 * P * k + P * t + P], yt[:, t, P * k:P * k + P], identf[:, :])
                last.then_inc(tpe, 1)

            def t_up(tt, r, alone=False):
                if r == 0:
                    pe.wait_ge(ffn_w, 3)
                    pe.wait_ge(tdve, ND * tt + DV["x1lo"])
                else:
                    pe.wait_ge(tdve, ND * tt + DV[f"y2{r - 1}"])
                if r == 2 and not alone:
                    pe.wait_ge(proj_lo, 16 * (tt + TAIL_LAG + 1) + 8)
                for wt, bk in ((Wg, misc[0]), (Wu, misc[1])):
                    for q in range(2):
                        m = 2 * r + q
                        n = 0
                        for k in range(KD):
                            for xx in (x1h, x1l):
                                last = mm(bk[:, 2 * P * q:2 * P * q + 2 * P], wt[:, k, P * m:P * m + P], xx[:, k, :],
                                          start=(n == 0), stop=(n == 2 * KD - 1))
                                n += 1
                    last.then_inc(tpe, 1)

            def t_down(tt, r):
                pe.wait_ge(tpool, NP * tt + PL[f"hl{r}"])
                for t in range(2):
                    n = 0
                    for q in range(2):
                        for hx in (hh, hl):
                            last = mm(misc[0][:, D * t:D * t + D], hx[:, q, P * t:P * t + P], Wd[:, 2 * r + q, :],
                                      start=(n == 0), stop=(n == 3))
                            n += 1
                last.then_inc(tpe, 1)

            def pair_ready(it, pair):
                pe.wait_ge(proj_lo, 16 * it + 8 * pair + 8)
                pe.wait_ge(qk_dup[pair], 64 * (it + 1))

            def iteration(it, first=False, tail=False, last=False):
                nxt = it + 1
                for u in range(4):
                    proj(it, 1, u)
                    if not first and u < LAG:
                        pv(it - 1, NST - LAG + u)
                for u in range(4):
                    v_unit(it, u)
                    for k in range(3 * u, 3 * u + 3):
                        max_chunk(it, 1, k)
                max_transpose(it, 1)
                pair_ready(it, 1)
                pe.wait_ge(v_lo, 8 * (it + 1))
                for s in range(NST):
                    scores(it, s)
                    if s in MAX_AT:
                        max_chunk(it, *MAX_AT[s])
                    if s in MAXT_AT:
                        max_transpose(it, MAXT_AT[s])
                    if s >= LAG:
                        pv(it, s - LAG)
                    if s in WO_AT and not first:
                        wo_unit(it - 1, WO_AT.index(s))
                    if not last:
                        if s in PROJ_AT:
                            proj(nxt, 0, PROJ_AT.index(s), y_at=4 * it, tail=tail)
                        if s in MAX_NEXT_AT:
                            if MAX_NEXT_AT[s] == 0:
                                pair_ready(nxt, 0)
                            max_chunk(nxt, 0, MAX_NEXT_AT[s])
                        if s == MAXT_NEXT_AT:
                            max_transpose(nxt, 0)
                    if tail:
                        tt = it - TAIL_LAG
                        if s == T_TR:
                            t_transpose(tt)
                        if s in T_UP:
                            t_up(tt, T_UP.index(s), alone=last)
                        if s in T_DOWN:
                            t_down(tt, T_DOWN.index(s))

            for u in range(4):
                proj(0, 0, u, first=True)
            pe.wait_ge(const_b, 3)
            pe.wait_ge(buf_init, 14)
            pair_ready(0, 0)
            for k in range(NC):
                max_chunk(0, 0, k)
            max_transpose(0, 0)
            iteration(0, first=True)
            with pe.Fori(1, TAIL_LAG) as it:
                iteration(it)
            with pe.Fori(TAIL_LAG, NIT - 1) as it:
                iteration(it, tail=True)
            iteration(NIT - 1, tail=True, last=True)
            for s in range(NST - LAG, NST):
                pv(NIT - 1, s)
            pe.wait_ge(tdve, ND * (NIT - TAIL_LAG))
            for u in range(4):
                wo_unit(NIT - 1, u, alone=True)
            pe.wait_ge(y_added, 4 * NIT)
            with pe.Fori(NIT - TAIL_LAG, NIT) as tt:
                t_transpose(tt, alone=True)
                for r in range(3):
                    t_up(tt, r, alone=True)
                    t_down(tt, r)

        @block.scalar
        def _(act):
            A = nc.scalar.activation

            def stage(nxt, p):
                act.wait_ge(raw_loaded, 16 * (4 * nxt + p + 1))
                if p == 0:
                    if started(4 * nxt):
                        act.wait_ge(v_mm, 4 * nxt)
                if p < KD:
                    A(xh[:, p, :], raw[:, :], ACT.Copy).then_inc(raw_hi, 1)
                else:
                    A(wh[:, p - KD, :], raw[:, 0:WC], ACT.Copy).then_inc(raw_hi, 1)

            def proj_evac(it, pair, u):
                c, kind = u % 2, u // 2
                act.wait_ge(proj_mm, 8 * it + 4 * pair + u + 1)
                used = NST * (it - 1) + 2 * NS * (pair + 1)
                if u == 0 and started(used):
                    act.wait_ge(st_mm, used)
                dst = (Q1, K1)[kind]
                sc = SCALE if kind == 0 else 1.0
                for hd, rows in ((0, slice(0, E)), (1, slice(E, P))):
                    A(dst[rows, 2 * pair + hd, CH * c:CH * c + CH], misc[u % 2][rows, :], ACT.Copy, scale=sc).then_inc(proj_hi, 1)

            def v_evac(it, u):
                act.wait_ge(v_mm, 4 * it + u + 1)
                if u == 0:
                    if started(NST * it):
                        act.wait_ge(pv_mm, NST * it)
                for t in range(2):
                    dst = VH[:, 2 * u + t, :, :].rearrange("p r (a e) -> p r a e", e=E)[:, :, 0:3:2, :]
                    src = misc[u % 2][:, 2 * P * t:2 * P * t + 2 * P].rearrange("p (r a e) -> p r a e", r=2, a=2)
                    A(dst, src, ACT.Copy).then_inc(v_hi, 1)

            def exp(it, s):
                i, c = STEPS[s % NS]
                o, _ = step_cols(i, c)
                if started(NST * it + s - 1):
                    act.wait_ge(*lo_of(it, s - 2))
                act.wait_ge(st_mm, NST * it + s + 1)
                A(pe_[:, s % 2, o:CH], stb[s % 2][:, o:CH], ACT.Exp).then_inc(exp_done, 1)
                if started(NST * it + s - RING + 1):
                    act.wait_ge(pv_mm, NST * it + s - RING + 1)
                A(ph[:, s % RING, o:CH], stb[s % 2][:, o:CH], ACT.Exp).then_inc(hi_done, 1)

            def copy_out(it, n, c):
                act.wait_ge(pv_mm, NST * it + NS * n + (4 if c == 0 else NS))
                if n < 2 and c == 0:
                    if started(4 * it):
                        act.wait_ge(wo_mm, 4 * it)
                if c == 0:
                    if started(16 * (QH * it + n - 1)):
                        act.wait_ge(sums_loaded, 16 * (QH * it + n - 1))
                rows, srow = (slice(0, E), E) if n % 2 == 0 else (slice(E, P), 0)
                cols = slice(CH * c, CH * c + CH)
                A(HT[rows, n // 2, cols], pvb[c][rows, :], ACT.Copy)
                A(rsum[srow:srow + 1, cols], pvb[c][srow:srow + 1, :], ACT.Copy).then_inc(ht_copied, 1)

            def t_x1(tt):
                act.wait_ge(tpe, NPE * tt + PEC["tr"])
                A(x1h[:, :, :], misc[0][:, :].rearrange("p (k n) -> p k n", k=KD), ACT.Copy).then_inc(tact, 1)

            def t_tanh(tt, r):
                act.wait_ge(tpe, NPE * tt + PEC[f"u{r}"])
                if r:
                    act.wait_ge(tpool, NP * tt + PL[f"hl{r - 1}"])
                A(th[:, :, :], misc[0][:, :].rearrange("p (k n) -> p k n", k=2), ACT.Tanh, scale=0.5 * WSCALE).then_inc(tact, 1)

            def t_hh(tt, r):
                act.wait_ge(tdve, ND * tt + DV[f"h{r}"])
                if r:
                    act.wait_ge(tpe, NPE * tt + PEC[f"d{r - 1}"])
                A(hh[:, :, :], th[:, :, :], ACT.Copy).then_inc(tact, 1)

            def iteration(it, first=False, tail=False, last=False):
                nxt = it + 1
                for u in range(4):
                    proj_evac(it, 1, u)
                if not first:
                    copy_out(it - 1, QH - 1, 1)
                for u in range(4):
                    v_evac(it, u)
                for s in range(NST):
                    exp(it, s)
                    if s in COPY_AT:
                        copy_out(it, *COPY_AT[s])
                    if not last:
                        if s in STAGE_AT:
                            stage(nxt, STAGE_AT.index(s))
                        if s - 1 in PROJ_AT:
                            proj_evac(nxt, 0, PROJ_AT.index(s - 1))
                    if tail:
                        tt = it - TAIL_LAG
                        if s == T_X1S:
                            t_x1(tt)
                        if s in T_GATE:
                            t_tanh(tt, T_GATE.index(s))
                        if s in T_HS:
                            t_hh(tt, T_HS.index(s))

            for p in range(4):
                stage(0, p)
            for u in range(4):
                proj_evac(0, 0, u)
            iteration(0, first=True)
            with act.Fori(1, TAIL_LAG) as it:
                iteration(it)
            with act.Fori(TAIL_LAG, NIT - 1) as it:
                iteration(it, tail=True)
            iteration(NIT - 1, tail=True, last=True)
            copy_out(NIT - 1, QH - 1, 1)
            with act.Fori(NIT - TAIL_LAG, NIT) as tt:
                t_x1(tt)
                for r in range(3):
                    t_tanh(tt, r)
                    t_hh(tt, r)

        @block.vector
        def _(dve):
            V = nc.vector

            def proj_rest(it, pair, u):
                c, kind = u % 2, u // 2
                n = 16 * it + 8 * pair + 2 * u
                cols = slice(CH * c, CH * c + CH)
                for hd, rows in ((0, slice(0, E)), (1, slice(E, P))):
                    hx = 2 * pair + hd
                    dve.wait_ge(proj_hi, n + hd + 1)
                    if kind == 0:
                        V.scalar_tensor_tensor(Q2[rows, hx, cols], misc[u % 2][rows, :], SCALE,
                                               Q1[rows, hx, cols].bitcast(F32), ALU.mult, ALU.subtract).then_inc(proj_lo, 1)
                    else:
                        other = slice(E, P) if hd == 0 else slice(0, E)
                        V.tensor_tensor(K1[other, hx, cols], misc[u % 2][rows, :],
                                        K1[rows, hx, cols].bitcast(F32), ALU.subtract).then_inc(proj_lo, 1)

            def v_rest(it, u):
                dve.wait_ge(v_hi, 8 * it + 2 * u + 2)
                for t in range(2):
                    def part(X):
                        return X[:, 2 * u + t, :, :].rearrange("p r (a e) -> p r a e", e=E)[:, :, 0:3:2, :]
                    src = misc[u % 2][:, 2 * P * t:2 * P * t + 2 * P].rearrange("p (r a e) -> p r a e", r=2, a=2)
                    V.tensor_tensor(part(VL), src, part(VH).bitcast(F32), ALU.subtract).then_inc(v_lo, 1)

            def max_chunk(it, n, k):
                e = RING_AT["c", n, k]
                dve.wait_ge(mx_mm, NMX * it + e + 1)
                if k == 0:
                    if started(NMX * it + (RING_AT["t", n - 2, 0] + 1 if n >= 2 else 0)):
                        dve.wait_ge(mx_mm, NMX * it + (RING_AT["t", n - 2, 0] + 1 if n >= 2 else 0))
                j, c = CHUNKS[k]
                width = min(CH, P * (j + 1) - CH * c)
                at = j if c == 0 else TT + j - 4
                V.reduce_max(mp[:, n % 2, at:at + 1], mxb[e % 2][:, 0:width], AX.X).then_inc(mx_read, 1)
                if k == NC - 1:
                    dve.wait_ge(mx_read, NMX * it + e + 1)
                    V.tensor_tensor(mp[:, n % 2, 4:TT], mp[:, n % 2, 4:TT], mp[:, n % 2, TT:NC], ALU.max).then_inc(mx_comb, 1)

            def max_row8(it, n):
                e = RING_AT["t", n, 0]
                dve.wait_ge(mx_mm, NMX * it + e + 1)
                if n >= 2:
                    dve.wait_ge(max_row[n - 2], 16 * (it + 1))
                else:
                    if started(16 * it):
                        dve.wait_ge(max_row[n + 2], 16 * it)
                V.tensor_scalar(M8[:, n % 2, :], mxb[e % 2][0:TT, 0:P], -1.0, None, ALU.mult).then_inc(mx_read, 1)

            def probs_lo(it, s):
                i, c = STEPS[s % NS]
                o, _ = step_cols(i, c)
                dve.wait_ge(hi_done, NST * it + s + 1)
                V.tensor_tensor(pl[:, s % RING, o:CH], pe_[:, s % 2, o:CH], ph[:, s % RING, o:CH].bitcast(F32),
                                ALU.subtract).then_inc(lo_dve, 1)

            def recip(it, n):
                k = QH * it + n
                dve.wait_ge(sums_loaded, 16 * (k + 1))
                if started(16 * k):
                    dve.wait_ge(recip_stored, 16 * k)
                if started(2 * it + n // 2):
                    dve.wait_ge(ht_norm, 2 * it + n // 2)
                V.reciprocal(R64[:, :], S64[:, :]).then_inc(recip_done, 1)

            def y_add(wi, u, seq):
                dve.wait_ge(wo_mm, 4 * wi + u + 1)
                if u == 0:
                    dve.wait_ge(y_inited, 16 * (seq + 1))
                yy = y[:, 2 * u:2 * u + 2, :]
                V.tensor_tensor(yy, misc[u % 2][:, :].rearrange("p (t d) -> p t d", t=2), yy, ALU.add).then_inc(y_added, 1)

            def own(tt, key):
                dve.wait_ge(tdve, ND * tt + DV[key])

            def stats(tt, x2, keys):
                for t in range(2):
                    V.bn_stats(st[:, t, :], x2[:, t, :]).then_inc(tdve, 1)
                own(tt, keys[1])
                V.memset(carrier[:, :], 0.0)
                for t in range(2):
                    V.bn_aggr(mv[:, t, :], st[:, t, :]).then_inc(tdve, 1)

            def normalise(tt, x2, key):
                dve.wait_ge(tpool, NP * tt + PL[key])
                for t in range(2):
                    V.tensor_scalar(x2[:, t, :], x2[:, t, :], mv[:, t, 0:1], rs[:, t:t + 1], ALU.subtract, ALU.mult).then_inc(tdve, 1)

            def t_ln1(tt):
                dve.wait_ge(tail_loaded, 32 * (tt + 1))
                stats(tt, yt, ["st1a", "st1b"])

            def t_add(tt):
                dve.wait_ge(tpool, NP * tt + PL["gam"])
                V.tensor_tensor(yt[:, :, :], yt[:, :, :], xt[:, :, :], ALU.add).then_inc(tdve, 1)
                own(tt, "add")
                stats(tt, yt, ["st2a", "st2b"])

            def t_x1lo(tt):
                dve.wait_ge(tact, NA * tt + AC["x1hi"])
                V.tensor_tensor(x1l[:, :, :], misc[0][:, :].rearrange("p (k n) -> p k n", k=KD),
                                x1h[:, :, :].bitcast(F32), ALU.subtract).then_inc(tdve, 1)

            def t_glu(tt, r):
                dve.wait_ge(tact, NA * tt + AC[f"tanh{r}"])
                V.scalar_tensor_tensor(th[:, :, :], th[:, :, :], 1.0, misc[0][:, :].rearrange("p (k n) -> p k n", k=2),
                                       ALU.add, ALU.mult).then_inc(tdve, 1)
                own(tt, f"tg{r}")
                V.tensor_tensor(th[:, :, :], misc[1][:, :].rearrange("p (k n) -> p k n", k=2), th[:, :, :], ALU.mult).then_inc(tdve, 1)

            def t_y2(tt, r):
                dve.wait_ge(tpe, NPE * tt + PEC[f"d{r}"])
                if r:
                    own(tt, f"y2{r - 1}")
                V.scalar_tensor_tensor(yt[:, :, :], misc[0][:, :].rearrange("p (t d) -> p t d", t=2), 0.5 * WSCALE ** 3,
                                       yt[:, :, :], ALU.mult, ALU.add).then_inc(tdve, 1)

            def t_ln3(tt):
                own(tt, "y22")
                stats(tt, yt, ["st3a", "st3b"])

            def iteration(it, first=False, tail=False, last=False):
                nxt = it + 1
                for u in range(4):
                    proj_rest(it, 1, u)
                for u in range(4):
                    v_rest(it, u)
                    for k in range(3 * u, 3 * u + 3):
                        max_chunk(it, 1, k)
                    if u == 1 and not first:
                        recip(it - 1, QH - 1)
                max_row8(it, 1)
                for s in range(NST):
                    if s % LO_VECTOR == LO_VECTOR - 1:
                        probs_lo(it, s)
                    if s in MAX_AT:
                        max_chunk(it, *MAX_AT[s])
                    if s in MAXT_AT:
                        max_row8(it, MAXT_AT[s])
                    if s in RECIP_AT:
                        recip(it, RECIP_AT[s])
                    if s - 1 in WO_AT and not first:
                        y_add(it - 1, WO_AT.index(s - 1), (it - 1) // NQ)
                    if not last:
                        if s - 1 in PROJ_AT:
                            proj_rest(nxt, 0, PROJ_AT.index(s - 1))
                        if s in MAX_NEXT_AT:
                            max_chunk(nxt, 0, MAX_NEXT_AT[s])
                        if s == MAXT_NEXT_AT:
                            max_row8(nxt, 0)
                    if tail:
                        tt = it - TAIL_LAG
                        if s == T_LN1:
                            t_ln1(tt)
                        if s == T_LN1N:
                            normalise(tt, yt, "r1")
                        if s == T_ADD:
                            t_add(tt)
                        if s == T_X1:
                            normalise(tt, yt, "r2")
                        if s == T_X1S:
                            t_x1lo(tt)
                        if s in T_GATE:
                            t_glu(tt, T_GATE.index(s))
                        if s in T_Y2:
                            t_y2(tt, T_Y2.index(s))
                        if s == T_LN3:
                            t_ln3(tt)
                        if s == T_OUT:
                            normalise(tt, yt, "r3")

            V.memset(VH[:, :, :, E:2 * E].bitcast(F32), 1.0).then_inc(buf_init, 1)
            V.memset(VL[:, :, :, E:2 * E].bitcast(F32), 0.0).then_inc(buf_init, 1)
            for pair in range(2):
                a, b = 2 * pair, 2 * pair + 1
                for X in (Q2, K2):
                    V.memset(X[E:P, a, :].bitcast(F32), 0.0).then_inc(buf_init, 1)
                    V.memset(X[0:E, b, :].bitcast(F32), 0.0).then_inc(buf_init, 1)
            dve.wait_ge(buf_init, 10)
            for pair in range(2):
                V.memset(K2[E:E + 1, 2 * pair, :].bitcast(F32), 1.0).then_inc(buf_init, 1)
                V.memset(K2[0:1, 2 * pair + 1, :].bitcast(F32), 1.0).then_inc(buf_init, 1)
            dve.wait_ge(const_step, 8)
            V.tensor_copy(maskT[:, :], mraw[:, 0:2 * P]).then_inc(const_b, 1)
            V.tensor_copy(maskS[:, :], mraw[:, 2 * P:3 * P]).then_inc(const_b, 1)
            V.tensor_copy(identb[:, :], identf[:, :]).then_inc(const_b, 1)
            for u in range(4):
                proj_rest(0, 0, u)
            for k in range(NC):
                max_chunk(0, 0, k)
            max_row8(0, 0)
            iteration(0, first=True)
            with dve.Fori(1, TAIL_LAG) as it:
                iteration(it)
            with dve.Fori(TAIL_LAG, NIT - 1) as it:
                iteration(it, tail=True)
            iteration(NIT - 1, tail=True, last=True)
            recip(NIT - 1, QH - 1)
            for u in range(4):
                y_add(NIT - 1, u, B - 1)
            with dve.Fori(NIT - TAIL_LAG, NIT) as tt:
                t_ln1(tt)
                normalise(tt, yt, "r1")
                t_add(tt)
                normalise(tt, yt, "r2")
                t_x1lo(tt)
                for r in range(3):
                    t_glu(tt, r)
                    t_y2(tt, r)
                t_ln3(tt)
                normalise(tt, yt, "r3")

        @block.gpsimd
        def _(pool):
            G = nc.gpsimd

            def stage(nxt, p):
                pool.wait_ge(raw_hi, 4 * nxt + p + 1)
                if p < KD:
                    G.tensor_tensor(xl[:, p, :], raw[:, :], xh[:, p, :].bitcast(F32), ALU.subtract).then_inc(raw_split, 1)
                else:
                    G.tensor_tensor(wl[:, p - KD, :], raw[:, 0:WC], wh[:, p - KD, :].bitcast(F32), ALU.subtract).then_inc(raw_split, 1)

            def probs_lo(it, s):
                i, c = STEPS[s % NS]
                o, _ = step_cols(i, c)
                pool.wait_ge(hi_done, NST * it + s + 1)
                G.tensor_tensor(pl[:, s % RING, o:CH], pe_[:, s % 2, o:CH], ph[:, s % RING, o:CH].bitcast(F32),
                                ALU.subtract).then_inc(lo_pool, 1)

            def norm(it, pair):
                pool.wait_ge(recip_bc, 16 * (QH * it + 2 * pair + 2))
                G.tensor_tensor(HT[:, pair, :], HT[:, pair, :], RB[:, :], ALU.mult).then_inc(ht_norm, 1)

            def own(tt, key):
                pool.wait_ge(tpool, NP * tt + PL[key])

            def rstd(tt, eps, dkey, ekey):
                pool.wait_ge(tdve, ND * tt + DV[dkey])
                G.tensor_tensor(rs[:, :], mv[:, :, 1:2].rearrange("p t o -> p (t o)"), eps[:, :], ALU.add).then_inc(tpool, 1)
                own(tt, ekey)
                G.tensor_tensor(rs[:, :], rs[:, :], halves[:, :], ALU.pow).then_inc(tpool, 1)

            def t_xb(tt):
                pool.wait_ge(tail_loaded, 32 * (tt + 1))
                pool.wait_ge(consts_loaded, 32)
                G.tensor_tensor(xt[:, :, :], xt[:, :, :], bt[:, :].rearrange("p (o d) -> p o d", o=1).broadcast_to([P, 2, D]), ALU.add).then_inc(tpool, 1)

            def t_gamma(tt):
                pool.wait_ge(tdve, ND * tt + DV["n1b"])
                G.tensor_tensor(yt[:, :, :], yt[:, :, :], gm[:, :].rearrange("p (o d) -> p o d", o=1).broadcast_to([P, 2, D]), ALU.mult).then_inc(tpool, 1)

            def t_hl(tt, r):
                pool.wait_ge(tact, NA * tt + AC[f"hh{r}"])
                G.tensor_tensor(hl[:, :, :], th[:, :, :], hh[:, :, :].bitcast(F32), ALU.subtract).then_inc(tpool, 1)

            def iteration(it, first=False, tail=False, last=False):
                if not first:
                    norm(it - 1, 1)
                for s in range(NST):
                    if s % LO_VECTOR < LO_VECTOR - 1:
                        probs_lo(it, s)
                    if s in STAGE_AT and not last:
                        stage(it + 1, STAGE_AT.index(s))
                    if s == NORM_AT:
                        norm(it, 0)
                    if tail:
                        tt = it - TAIL_LAG
                        if s == T_LN1:
                            t_xb(tt)
                        if s == T_LN1R:
                            rstd(tt, eps_attn, "mv1b", "e1")
                        if s == T_AFF:
                            t_gamma(tt)
                        if s == T_LN2R:
                            rstd(tt, eps_ln, "mv2b", "e2")
                        if s in T_HL:
                            t_hl(tt, T_HL.index(s))
                        if s == T_LN3R:
                            rstd(tt, eps_ln, "mv3b", "e3")

            G.memset(identf[:, :], 0.0).then_inc(const_step, 1)
            G.memset(mraw[:, :], 0.0).then_inc(const_step, 1)
            G.memset(halves[:, :], -0.5).then_inc(const_step, 1)
            G.memset(eps_attn[:, :], LN_EPS_ATTN).then_inc(const_step, 1)
            G.memset(eps_ln[:, :], LN_EPS).then_inc(const_step, 1)
            pool.wait_ge(const_step, 5)
            G.affine_select(out=identf[:, :], in_=identf[:, :], compare_op=ALU.not_equal, fill=1.0, base=0,
                            pattern=[[-1, P]], channel_multiplier=1).then_inc(const_step, 1)
            G.affine_select(out=mraw[:, 0:2 * P], in_=mraw[:, 0:2 * P], compare_op=ALU.is_ge, fill=MASKED, base=-P,
                            pattern=[[1, 2 * P]], channel_multiplier=-1).then_inc(const_step, 1)
            G.affine_select(out=mraw[:, 2 * P:3 * P], in_=mraw[:, 2 * P:3 * P], compare_op=ALU.is_ge, fill=MASKED, base=0,
                            pattern=[[-1, P]], channel_multiplier=1).then_inc(const_step, 1)
            for p in range(4):
                stage(0, p)
            for n, wt in enumerate((Wg, Wu, Wd)):
                pool.wait_ge(ffn_raw, 16 * (n + 1))
                dst = wt[:, :, :] if n < 2 else wt[:, :, :].rearrange("p (a b) d -> p a (b d)", a=2)
                G.tensor_copy(dst, HT[:, :, 0:HID].bitcast(I32)).then_inc(ffn_w, 1)
            iteration(0, first=True)
            with pool.Fori(1, TAIL_LAG) as it:
                iteration(it)
            with pool.Fori(TAIL_LAG, NIT - 1) as it:
                iteration(it, tail=True)
            iteration(NIT - 1, tail=True, last=True)
            norm(NIT - 1, 1)
            with pool.Fori(NIT - TAIL_LAG, NIT) as tt:
                t_xb(tt)
                rstd(tt, eps_attn, "mv1b", "e1")
                t_gamma(tt)
                rstd(tt, eps_ln, "mv2b", "e2")
                for r in range(3):
                    t_hl(tt, r)
                rstd(tt, eps_ln, "mv3b", "e3")


def kernel(L0_attn_x, L0_attn_Wq, L0_attn_Wk, L0_attn_Wv, L0_attn_Wo, L0_attn_gamma, L0_attn_beta,
           L0_ffn_w_gate, L0_ffn_w_up, L0_ffn_w_down):
    import numpy as np
    import concourse.bacc as bacc
    from concourse.bass_utils import run_bass_kernel_spmd as run

    x = np.ascontiguousarray(L0_attn_x)
    w3 = np.stack([np.asarray(a) for a in (L0_attn_Wq, L0_attn_Wk, L0_attn_Wv)])
    w3 = w3.reshape(3, NQ, QH, KD, P, E).transpose(1, 3, 4, 0, 2, 5).reshape(NQ, KD, P, 3 * QH * E)
    arrays = {
        "xT": x.transpose(0, 2, 1).reshape(B, KD, P, S),
        "x": x,
        "wqkv": w3,
        "wo": np.asarray(L0_attn_Wo).reshape(NQ, 2, P, D),
        "w_gate_T": np.asarray(L0_ffn_w_gate).T.reshape(KD, P, HID).transpose(1, 0, 2),
        "w_up_T": np.asarray(L0_ffn_w_up).T.reshape(KD, P, HID).transpose(1, 0, 2),
        "w_down_T": np.asarray(L0_ffn_w_down).T.reshape(NH6, P, D).transpose(1, 0, 2).reshape(P, 2, HID),
        "gamma": np.asarray(L0_attn_gamma).reshape(1, D),
        "beta": np.asarray(L0_attn_beta).reshape(1, D),
    }
    arrays = {k: np.ascontiguousarray(a) for k, a in arrays.items()}
    nc = bacc.Bacc("TRN2", target_bir_lowering=False, num_devices=1)
    aps = {k: nc.dram_tensor(k, a.shape, mybir.dt.from_np(a.dtype), kind="ExternalInput").ap() for k, a in arrays.items()}
    out = nc.dram_tensor("out", (B, S, D), F32, kind="ExternalOutput").ap()
    yscr = nc.dram_tensor("y_scratch", (S, D), F32, kind="Internal").ap()
    rscr = nc.dram_tensor("recip_scratch", (QH, S), F32, kind="Internal").ap()
    build(nc, aps["xT"], aps["x"], aps["wqkv"], aps["wo"], aps["w_gate_T"], aps["w_up_T"], aps["w_down_T"],
          aps["gamma"], aps["beta"], out, yscr, rscr)
    r = run(nc, [arrays], core_ids=[0])
    return r.results[0]["out"]
```

```python
import concourse.bass as bass
from concourse import mybir
from collections import namedtuple
from contextlib import ExitStack

F32 = mybir.dt.float32
F32R = mybir.dt.float32r
BF16 = mybir.dt.bfloat16
I32 = mybir.dt.int32
ALU = mybir.AluOpType
ACT = mybir.ActivationFunctionType
AX = mybir.AxisListType

P = 128
B, S, D = 4, 1024, 256
H, E = 16, 64
HID = 768
KD = D // P
QH = 4
NQ = H // QH
NIT = B * NQ
TT = S // P
CH = 512
NH6 = HID // P
LN_EPS_ATTN = 1e-3
LN_EPS = 1e-5
SCALE = float(E) ** -0.5
WSCALE = 1.0 / 127.0
MASKED = -1e30

STEPS = [(i, c) for c in range(S // CH) for i in range(4 * (c + 1))]
NS = len(STEPS)
NST = QH * NS
CHUNKS = [(j, c) for j in range(TT) for c in range(j // 4 + 1)]
NC = len(CHUNKS)
NMX = QH * (NC + 1)
LAG = 3
RING = 4


def step_cols(i, c):
    lo = max(0, P * i - CH * c)
    return min(lo, CH - 2 * P), lo


RING_ORDER = ([("c", 0, k) for k in range(NC)] + [("t", 0, 0)] + [("c", 1, k) for k in range(NC)]
              + [("c", 2, 0), ("t", 1, 0)] + [("c", 2, k) for k in range(1, NC)]
              + [("c", 3, k) for k in range(3)] + [("t", 2, 0)] + [("c", 3, k) for k in range(3, NC)] + [("t", 3, 0)])
RING_AT = {e: n for n, e in enumerate(RING_ORDER)}

MAX_AT = {s: (2 + s // NS, s % NS) for s in range(2 * NS)}
MAX_NEXT_AT = {36 + k: k for k in range(NC)}
MAX1_BY_PROJ, MAX1_BY_V = [[0], [1], [2], [3]], [[4], [5, 6, 7], [8, 9], [10, 11]]
MAXT_AT = {1: 1, 14: 2, 26: 3}
WO_AT = [2, 3, 5, 6]
PROJ_AT = [27, 28, 30, 32]
STAGE_AT = [5, 11, 17, 20]
COPY_AT = {12 * n + 7: (n, 0) for n in range(QH)} | {12 * n + 15: (n, 1) for n in range(QH - 1)}
RECIP_AT = {12 * n + 20: n for n in range(QH - 1)}
NORM_AT = 40
def tail_at(ln1, ln1r, ln1n, aff, add, ln2r, x1, tr, rounds, ln3):
    return dict(LN1=ln1, LN1R=ln1r, LN1N=ln1n, AFF=aff, ADD=add, LN2R=ln2r, X1=x1, TR=tr, X1S=tr + 1,
                UP=rounds, GATE=[a + 1 for a in rounds], HS=[a + 2 for a in rounds], DOWN=[a + 5 for a in rounds],
                Y2=[a + 6 for a in rounds], LN3=ln3, LN3R=ln3 + 1, OUT=ln3 + 2)


STEADY = tail_at(0, 1, 2, 4, 5, 6, 8, 12, [14, 21, 35], 42)
LAST_A = tail_at(0, 1, 2, 4, 5, 6, 8, 12, [14, 21, 28], 35)
LAST_B = tail_at(1, 2, 3, 5, 7, 8, 10, 27, [28, 35, 42], 48)
TAIL_LAG = NQ + 1
XTRA = NIT - TAIL_LAG
LO_VECTOR = 3


Tail = namedtuple("Tail", "yt xt x1h x1l th hh hl st mv rs bk")


def build(nc, xT, x, wqkv, wo, wg, wu, wd, gamma, beta, out, yscr, rscr):
    ctx = ExitStack()
    with ctx:
        def sb(name, shape, dt=F32):
            return ctx.enter_context(nc.sbuf_tensor(name, shape, dt))

        def sem(name):
            return ctx.enter_context(nc.semaphore(name))

        raw = sb("raw", [P, S])
        xh, xl = sb("xh", [P, KD, S], F32R), sb("xl", [P, KD, S], F32R)
        WC = 3 * QH * E
        wh, wl = sb("wh", [P, KD, WC], F32R), sb("wl", [P, KD, WC], F32R)
        Q1, Q2 = sb("Q1", [P, QH, S], F32R), sb("Q2", [P, QH, S], F32R)
        K1, K2 = sb("K1", [P, QH, S], F32R), sb("K2", [P, QH, S], F32R)
        VW = 3 * E
        VH, VL = sb("VH", [P, TT, 2, VW], F32R), sb("VL", [P, TT, 2, VW], F32R)
        pe_ = sb("probs", [P, 2, CH])
        ph, pl = sb("probs_hi", [P, RING, CH], F32R), sb("probs_lo", [P, RING, CH], F32R)
        HT = sb("heads_T", [P, 2, S])
        rsum = sb("row_sums", [P, S])
        RB = sb("recip_bc", [P, S])
        S64, R64 = sb("sums64", [E, S // E]), sb("recip64", [E, S // E])
        mp = sb("max_part", [P, 2, NC])
        M8 = sb("neg_max8", [TT, 2, P], F32R)
        WoS = sb("wo_quad", [P, 2, D])
        y = sb("y", [P, TT, D])
        Wg, Wu, Wd = sb("w_gate", [P, KD, HID], F32R), sb("w_up", [P, KD, HID], F32R), sb("w_down", [P, NH6, D], F32R)
        y_tail, x_tail = sb("y_tail", [P, 2, D]), sb("x_tail", [P, 2, D])
        x1h, x1l = sb("x1T_hi", [P, KD, 2 * P], F32R), sb("x1T_lo", [P, KD, 2 * P], F32R)
        th, hh, hl = sb("tanh_h", [P, 2, 2 * P]), sb("h_hi", [P, 2, 2 * P], F32R), sb("h_lo", [P, 2, 2 * P], F32R)
        th_x = sb("tanh_extra", [P, 2, 2 * P])
        gm, bt = sb("gamma_bc", [P, D]), sb("beta_bc", [P, D])
        st, mv, rs = sb("bn_st", [P, NQ + 1, 2, 6]), sb("mean_var", [P, NQ + 1, 2, 2]), sb("rstd", [P, NQ + 1, 2])
        halves, eps_attn, eps_ln = sb("minus_half", [P, 2]), sb("eps_attn", [P, 2]), sb("eps_ln", [P, 2])
        carrier = sb("carrier", [1, 1])
        identf, identb = sb("ident_f", [P, P]), sb("ident_b", [P, P], BF16)
        maskS = sb("mask_keys_free", [P, P], BF16)
        maskT = sb("mask_queries_free", [P, 2 * P], BF16)
        mraw = th[:, :, :].rearrange("p a b -> p (a b)")

        bank = [ctx.enter_context(nc.psum_tensor(f"bank{i}", [P, CH], F32)) for i in range(8)]
        misc, mxb, stb, pvb = bank[0:2], bank[2:4], bank[4:6], bank[6:8]

        def tail_set(g, bufs, bk):
            return Tail(*bufs, st[:, g, :, :], mv[:, g, :, :], rs[:, g, :], bk)

        def carved(X, n):
            flat = X[:, :, :].rearrange("p a b -> p (a b)")
            return [flat[:, CH * k:CH * k + CH].rearrange("p (a b) -> p a b", a=2) for k in range(n)]

        def halved(X):
            return [X[:, CH * k:CH * k + CH].rearrange("p (a b) -> p a b", a=2) for k in range(2)]

        T = [tail_set(0, [y_tail, x_tail, x1h, x1l, th, hh, hl], misc)]
        xts = [*halved(rsum), y_tail]
        ths = [pe_[:, 0, :].rearrange("p (a b) -> p a b", a=2), pe_[:, 1, :].rearrange("p (a b) -> p a b", a=2), th_x]
        for g, (X, bk) in enumerate(((Q1, mxb), (Q2, stb), (K1, pvb))):
            c = carved(X, 4)
            T.append(tail_set(g + 1, [None, xts[g], c[0], c[1], ths[g], c[2], c[3]], bk))
        c = carved(xh, 4)
        T.append(tail_set(NQ, [*halved(raw), c[0], c[1], th_x, c[2], c[3]], mxb))
        EXTRA = NQ

        def rows_of(g, final):
            return y[:, 2 * g:2 * g + 2, :] if final else T[g].yt[:, :, :]

        raw_loaded = sem("raw_loaded")
        qk_dup = [sem("qk_dup0"), sem("qk_dup1")]
        max_row = [sem(f"max_row{n}") for n in range(QH)]
        sums_loaded, recip_stored, recip_bc = sem("sums_loaded"), sem("recip_stored"), sem("recip_bc_loaded")
        wo_loaded, y_stored, y_inited = sem("wo_loaded"), sem("y_stored"), sem("y_inited")
        tail_loaded = [sem(f"tail_loaded{g}") for g in range(NQ + 1)]
        out_stored = sem("out_stored")
        ffn_raw, consts_loaded = sem("ffn_raw_loaded"), sem("consts_loaded")
        const_step, const_b = sem("const_step"), sem("const_bf16")
        buf_init = sem("buffers_initialised")
        ffn_w = sem("ffn_weights_ready")
        raw_hi, raw_split = sem("raw_hi_done"), sem("raw_split_done")
        proj_mm, proj_hi, proj_lo = sem("proj_mm"), sem("proj_hi"), sem("proj_lo")
        v_mm, v_hi, v_lo = sem("v_mm"), sem("v_hi"), sem("v_lo")
        mx_mm, mx_read, mx_comb = sem("max_scores"), sem("max_read"), sem("max_combined")
        st_mm, exp_done, hi_done, pv_mm = sem("scores_mm"), sem("exp_done"), sem("probs_hi_done"), sem("pv_mm")
        lo_dve, lo_pool = sem("probs_lo_vector"), sem("probs_lo_pool")
        ht_copied, recip_done, ht_norm = sem("heads_copied"), sem("recip_done"), sem("heads_normed")
        wo_mm, y_added = sem("wo_mm"), sem("y_added")
        tdve, tpool = [sem(f"tail_dve{g}") for g in range(NQ + 1)], [sem(f"tail_pool{g}") for g in range(NQ + 1)]
        tact, tpe = [sem(f"tail_act{g}") for g in range(NQ + 1)], [sem(f"tail_pe{g}") for g in range(NQ + 1)]

        def started(v):
            assert isinstance(v, int) or v.min_val > 0, "a register's value has to be positive"
            return not isinstance(v, int) or v > 0

        DV = {k: n + 1 for n, k in enumerate(
            ["st1a", "st1b", "mv1a", "mv1b", "n1a", "n1b", "add", "st2a", "st2b", "mv2a", "mv2b", "x1a", "x1b", "x1lo"]
            + [f"{k}{r}" for r in range(3) for k in ("tg", "h", "hh", "y2")]
            + ["st3a", "st3b", "mv3a", "mv3b", "oa", "ob"])}
        PL = {k: n + 1 for n, k in enumerate(
            ["xb", "e1", "r1", "gam", "e2", "r2", "hl0", "hl1", "hl2", "e3", "r3"])}
        AC = {k: n + 1 for n, k in enumerate(["x1hi", "tanh0", "tanh1", "tanh2"])}
        PEC = {k: n + 1 for n, k in enumerate(["tr", "g0", "u0", "d0", "g1", "u1", "d1", "g2", "u2", "d2"])}
        ND, NP, NA, NPE = len(DV), len(PL), len(AC), len(PEC)

        def lo_of(it, s):
            if s < 0:
                it, s = it - 1, s + NST
            if s % LO_VECTOR == LO_VECTOR - 1:
                return lo_dve, NST // LO_VECTOR * it + s // LO_VECTOR + 1
            return lo_pool, (NST - NST // LO_VECTOR) * it + s - s // LO_VECTOR + 1

        def finals(g):
            return XTRA if g == 0 else 0

        block = ctx.enter_context(nc.Block())

        @block.sync
        def _(sp):
            def bits(ap):
                return ap.bitcast(F32)

            def load_piece(nxt, p, seq_b, quad):
                if started(4 * nxt + p):
                    sp.wait_ge(raw_split, 4 * nxt + p)
                if not isinstance(nxt, int):
                    sp.wait_ge(raw_loaded, 1)
                if p < KD:
                    src = xT[bass.ds(seq_b, 1), p, :, :].rearrange("o p n -> (o p) n")
                    sp.dma_start(raw[:, :], src).then_inc(raw_loaded, 16)
                else:
                    src = wqkv[bass.ds(quad, 1), p - KD, :, :].rearrange("o p n -> (o p) n")
                    sp.dma_start(raw[:, 0:WC], src).then_inc(raw_loaded, 16)

            def dup(it, pair):
                a, b = 2 * pair, 2 * pair + 1
                sp.wait_ge(proj_hi, 16 * it + 8 * pair + 4)
                sp.dma_start(bits(Q1[E:P, a, :]), bits(Q1[0:E, a, :])).then_inc(qk_dup[pair], 16)
                sp.dma_start(bits(Q1[0:E, b, :]), bits(Q1[E:P, b, :])).then_inc(qk_dup[pair], 16)
                sp.wait_ge(proj_hi, 16 * it + 8 * pair + 8)
                sp.dma_start(bits(K2[0:E, a, :]), bits(K1[0:E, a, :])).then_inc(qk_dup[pair], 16)
                sp.dma_start(bits(K2[E:P, b, :]), bits(K1[E:P, b, :])).then_inc(qk_dup[pair], 16)

            def max_to_row(it, n):
                if isinstance(it, int) and it == 0:
                    sp.wait_ge(buf_init, 14)
                sp.wait_ge(mx_read, NMX * it + RING_AT["t", n, 0] + 1)
                row = E if n % 2 == 0 else 0
                sp.dma_start(bits(Q2[row:row + 1, n, :]).rearrange("o (j q) -> o j q", j=TT), bits(M8[:, n % 2, :]))\
                    .then_inc(max_row[n], 16)

            def sums(it, n):
                sp.wait_ge(ht_copied, 2 * QH * it + 2 * n + 2)
                row = E if n % 2 == 0 else 0
                sp.dma_start(S64[:, :], rsum[row:row + 1, :].rearrange("o (a b) -> o a b", a=E)).then_inc(sums_loaded, 16)

            def recips(it, n):
                k = QH * it + n
                sp.wait_ge(recip_done, k + 1)
                sp.dma_start(rscr[n:n + 1, :].rearrange("o (a b) -> (o a) b", a=E), R64[:, :]).then_inc(recip_stored, 16)
                sp.wait_ge(recip_stored, 16 * (k + 1))
                rows = slice(0, E) if n % 2 == 0 else slice(E, P)
                sp.dma_start(RB[rows, :], rscr[n:n + 1, :].partition_broadcast(E).rearrange("e o n -> e (o n)")
                             ).then_inc(recip_bc, 16)

            def y_turn(b):
                if not (isinstance(b, int) and b == 0):
                    sp.wait_ge(y_added, 16 * b)
                    sp.wait_ge(raw_loaded, 1)
                    sp.dma_start(yscr.rearrange("(t p) d -> p t d", p=P), y[:, :, :]).then_inc(y_stored, 16)
                    sp.wait_ge(y_stored, 16 * b)
                    sp.wait_ge(raw_loaded, 1)
                if not (isinstance(b, int) and b == B):
                    src = x[bass.ds(b, 1), :, :].rearrange("o (t p) d -> p (o t) d", p=P)
                    sp.dma_start(y[:, :, :], src).then_inc(y_inited, 16)

            def x_load(tt, g):
                src = x.rearrange("b (j t p) d -> (b j) p t d", p=P, t=2)[bass.ds(tt, 1)]
                sp.dma_start(T[g].xt[:, :, :], src.rearrange("o p t d -> (o p) t d")).then_inc(tail_loaded[g], 16)

            def tail_load(tt, g=0):
                if g == 0:
                    sp.wait_ge(out_stored, 16 * (tt + 1))
                    sp.wait_ge(raw_loaded, 1)
                else:
                    sp.wait_ge(raw_split, 4 * NIT)
                sp.dma_start(T[g].yt[:, :, :], yscr.rearrange("(j t p) d -> j p t d", p=P, t=2)[bass.ds(tt % NQ, 1)]
                             .rearrange("o p t d -> (o p) t d")).then_inc(tail_loaded[g], 16)
                x_load(tt, g)

            def tail_store(tt, n, g=0, final=False):
                sp.wait_ge(tdve[g], ND * n + DV["ob"])
                sp.wait_ge(raw_loaded, 1)
                dst = out.rearrange("b (j t p) d -> (b j) p t d", p=P, t=2)[bass.ds(tt, 1)]
                sp.dma_start(dst.rearrange("o p t d -> (o p) t d"), rows_of(g, final)).then_inc(out_stored, 16)

            def iteration(it, first=False, turn=None, tail=False, last=False):
                nxt = it + 1
                if tail:
                    tail_load(it - TAIL_LAG)
                dup(it, 1)
                if not first:
                    sums(it - 1, QH - 1)
                    recips(it - 1, QH - 1)
                max_to_row(it, 1)
                if last:
                    tail_load(XTRA, EXTRA)
                if not last:
                    for p in range(3):
                        load_piece(nxt, p, nxt // NQ, nxt % NQ)
                if turn is not None:
                    if tail:
                        sp.wait_ge(tail_loaded[0], 32 * (it - TAIL_LAG + 1))
                    y_turn(turn)
                max_to_row(it, 2)
                sums(it, 0)
                if not last:
                    load_piece(nxt, 3, nxt // NQ, nxt % NQ)
                if not first:
                    sp.wait_ge(wo_mm, 4 * it)
                    sp.wait_ge(raw_loaded, 1)
                sp.dma_start(WoS[:, :, :], wo[bass.ds(it % NQ, 1), :, :, :].rearrange("o r p d -> p (o r) d")).then_inc(wo_loaded, 16)
                recips(it, 0)
                max_to_row(it, 3)
                sums(it, 1)
                if not last:
                    dup(nxt, 0)
                recips(it, 1)
                sums(it, 2)
                if tail:
                    tail_store(it - TAIL_LAG, it - TAIL_LAG)
                recips(it, 2)
                if not last:
                    max_to_row(nxt, 0)

            sp.sem_inc(out_stored, 16)
            for p in range(4):
                load_piece(0, p, 0, 0)
            sp.dma_start(gm[:, :], gamma.partition_broadcast(P).rearrange("e o n -> e (o n)")).then_inc(consts_loaded, 16)
            sp.dma_start(bt[:, :], beta.partition_broadcast(P).rearrange("e o n -> e (o n)")).then_inc(consts_loaded, 16)
            sp.dma_start(HT[:, :, 0:HID].bitcast(I32), wg).then_inc(ffn_raw, 16)
            dup(0, 0)
            max_to_row(0, 0)
            sp.wait_ge(ffn_w, 1)
            sp.dma_start(HT[:, :, 0:HID].bitcast(I32), wu).then_inc(ffn_raw, 16)
            sp.wait_ge(ffn_w, 2)
            sp.dma_start(HT[:, :, 0:HID].bitcast(I32), wd).then_inc(ffn_raw, 16)
            iteration(0, first=True, turn=0)
            with sp.Fori(1, NQ) as it:
                iteration(it)
            for b in range(1, B):
                iteration(NQ * b, turn=b, tail=b > 1)
                with sp.Fori(NQ * b + 1, NQ * (b + 1) - (b == B - 1)) as it:
                    iteration(it, tail=True)
            iteration(NIT - 1, tail=True, last=True)
            sums(NIT - 1, QH - 1)
            sp.wait_ge(out_stored, 16 * (XTRA + 1))
            sp.wait_ge(sums_loaded, 16 * QH * NIT)
            for g in range(NQ):
                x_load(NIT - NQ + g, g)
            recips(NIT - 1, QH - 1)
            tail_store(XTRA, 0, EXTRA)
            for g in range(NQ):
                tail_store(NIT - NQ + g, finals(g), g, final=True)
            sp.wait_ge(out_stored, 16 * (NIT + 1))

        @block.tensor
        def _(pe):
            mm, tr = nc.tensor.matmul, nc.tensor.transpose

            def proj(it, pair, u, first=False, y_at=0, tail=False):
                n = 8 * it + 4 * pair + u
                if pair == 0 and u == 0 and not first:
                    pe.wait_ge(v_lo, 8 * it)
                    if started(y_at):
                        pe.wait_ge(y_added, y_at)
                    if tail:
                        pe.wait_ge(tdve[0], ND * (it - 1 - TAIL_LAG) + DV["y21"])
                if pair == 0 and u == 0:
                    pe.wait_ge(raw_split, 4 * (it + 1))
                if u >= 2 or pair == 1:
                    pe.wait_ge(proj_lo, 2 * n - 2)
                if pair == 1 and u == 0 and started(NST // LO_VECTOR * it):
                    pe.wait_ge(lo_dve, NST // LO_VECTOR * it)
                c, kind = u % 2, u // 2
                col = kind * QH * E + pair * 2 * E
                terms = [(wh, xh), (wh, xl), (wl, xh)]
                for k in range(KD):
                    for t, (a, b) in enumerate(terms):
                        last = mm(misc[u % 2][:, :], a[:, k, col:col + 2 * E], b[:, k, CH * c:CH * c + CH],
                                  start=(k == 0 and t == 0), stop=(k == KD - 1 and t == 2))
                last.then_inc(proj_mm, 1)

            def v_unit(it, u):
                if u < 2:
                    pe.wait_ge(proj_lo, 16 * it + 14 + 2 * u)
                else:
                    pe.wait_ge(v_lo, 8 * it + 2 * u - 2)
                col = 2 * QH * E
                for t in range(2):
                    tok = P * (2 * u + t)
                    n = 0
                    for k in range(KD):
                        for a, b in ((xh, wh), (xl, wh), (xh, wl)):
                            last = mm(misc[u % 2][:, 2 * P * t:2 * P * t + 2 * P], a[:, k, tok:tok + P],
                                      b[:, k, col:col + QH * E], start=(n == 0), stop=(n == 3 * KD - 1))
                            n += 1
                last.then_inc(v_mm, 1)

            def wo_unit(wi, u, alone=False):
                if u == 0:
                    pe.wait_ge(ht_norm, 2 * (wi + 1))
                    pe.wait_ge(wo_loaded, 16 * (wi + 1))
                if u < 2 and not alone:
                    pe.wait_ge(v_lo, 8 * wi + 14 + 2 * u)
                if u >= 2:
                    pe.wait_ge(y_added, 4 * wi + u - 1)
                for t in range(2):
                    tok = P * (2 * u + t)
                    for r in range(2):
                        last = mm(misc[u % 2][:, D * t:D * t + D], HT[:, r, tok:tok + P], WoS[:, r, :],
                                  start=(r == 0), stop=(r == 1))
                last.then_inc(wo_mm, 1)

            def max_chunk(it, n, k):
                e = RING_AT["c", n, k]
                if started(NMX * it + e - 1):
                    pe.wait_ge(mx_read, NMX * it + e - 1)
                j, c = CHUNKS[k]
                width = min(CH, P * (j + 1) - CH * c)
                diag = P * j - CH * c
                masked = diag < CH
                last = mm(mxb[e % 2][:, 0:width], Q1[:, n, P * j:P * j + P], K1[:, n, CH * c:CH * c + width],
                          start=True, stop=not masked)
                if masked:
                    last = mm(mxb[e % 2][:, diag:diag + P], identb[:, :], maskS[:, :], start=False, stop=True)
                last.then_inc(mx_mm, 1)

            def max_transpose(it, n):
                e = RING_AT["t", n, 0]
                pe.wait_ge(mx_read, NMX * it + e - 1)
                pe.wait_ge(mx_comb, QH * it + n + 1)
                tr(mxb[e % 2][0:TT, 0:P], mp[:, n % 2, 0:TT], identf[:, :]).then_inc(mx_mm, 1)

            def scores(it, s):
                n, (i, c) = s // NS, STEPS[s % NS]
                if started(NST * it + s - 1):
                    pe.wait_ge(hi_done, NST * it + s - 1)
                if s % NS == 0:
                    pe.wait_ge(max_row[n], 16 * (it + 1))
                o, lo = step_cols(i, c)
                q0 = CH * c
                mm(stb[s % 2][:, o:CH], K1[:, n, P * i:P * i + P], Q1[:, n, q0 + o:q0 + CH], start=True, stop=False)
                masked = P * i >= q0
                last = mm(stb[s % 2][:, o:CH], K2[:, n, P * i:P * i + P], Q2[:, n, q0 + o:q0 + CH],
                          start=False, stop=not masked)
                if masked:
                    last = mm(stb[s % 2][:, o:lo + P], identb[:, :], maskT[:, P - (lo - o):2 * P],
                              start=False, stop=True)
                last.then_inc(st_mm, 1)

            def pv(it, s):
                n, (i, c) = s // NS, STEPS[s % NS]
                if i == 0:
                    if started(2 * QH * it + 2 * n + c - 1):
                        pe.wait_ge(ht_copied, 2 * QH * it + 2 * n + c - 1)
                pe.wait_ge(*lo_of(it, s))
                o, _ = step_cols(i, c)
                v0 = 0 if n % 2 == 0 else E
                ops = [(VH, ph), (VH, pl), (VL, ph)]
                for t, (a, b) in enumerate(ops):
                    last = mm(pvb[c][:, o:CH], a[:, i, n // 2, v0:v0 + P], b[:, s % RING, o:CH],
                              start=(i == 0 and t == 0), stop=(i == 4 * c + 3 and t == 2))
                last.then_inc(pv_mm, 1)

            def t_transpose(n, g=0, it=None, final=False):
                pe.wait_ge(tdve[g], ND * n + DV["x1b"])
                if it is not None and g == 0:
                    pe.wait_ge(y_added, 4 * it)
                if g == EXTRA:
                    pe.wait_ge(mx_read, NMX * NIT)
                if final and g == 0:
                    pe.wait_ge(y_added, 4 * NIT)
                if final and g == 1:
                    pe.wait_ge(tdve[EXTRA], DV["y22"])
                if final and g == 2:
                    pe.wait_ge(hi_done, NST * NIT)
                if final and g == 3:
                    pe.wait_ge(ht_copied, 2 * QH * NIT)
                for k in range(KD):
                    for t in range(2):
                        last = tr(T[g].bk[0][:, 2 * P * k + P * t:2 * P * k + P * t + P],
                                  rows_of(g, final)[:, t, P * k:P * k + P], identf[:, :])
                last.then_inc(tpe[g], 1)

            def t_up(n, r, g=0, it=None):
                if r == 0:
                    pe.wait_ge(ffn_w, 3)
                    pe.wait_ge(tdve[g], ND * n + DV["x1lo"])
                else:
                    pe.wait_ge(tdve[g], ND * n + DV[f"y2{r - 1}"])
                if r == 2 and it is not None and g == 0:
                    pe.wait_ge(proj_lo, 16 * (it + 1) + 8)
                for wt, bk in ((Wg, T[g].bk[0]), (Wu, T[g].bk[1])):
                    for q in range(2):
                        m = 2 * r + q
                        cnt = 0
                        for k in range(KD):
                            for xx in (T[g].x1h, T[g].x1l):
                                last = mm(bk[:, 2 * P * q:2 * P * q + 2 * P], wt[:, k, P * m:P * m + P], xx[:, k, :],
                                          start=(cnt == 0), stop=(cnt == 2 * KD - 1))
                                cnt += 1
                    last.then_inc(tpe[g], 1)

            def t_down(n, r, g=0):
                pe.wait_ge(tpool[g], NP * n + PL[f"hl{r}"])
                for t in range(2):
                    cnt = 0
                    for q in range(2):
                        for hx in (T[g].hh, T[g].hl):
                            last = mm(T[g].bk[0][:, D * t:D * t + D], hx[:, q, P * t:P * t + P], Wd[:, 2 * r + q, :],
                                      start=(cnt == 0), stop=(cnt == 3))
                            cnt += 1
                last.then_inc(tpe[g], 1)

            def tail_step(n, g, s, at, it):
                if s == at["TR"]:
                    t_transpose(n, g, it)
                if s in at["UP"]:
                    t_up(n, at["UP"].index(s), g, it if at is STEADY else None)
                if s in at["DOWN"]:
                    t_down(n, at["DOWN"].index(s), g)

            def pair_ready(it, pair):
                pe.wait_ge(proj_lo, 16 * it + 8 * pair + 8)
                pe.wait_ge(qk_dup[pair], 64 * (it + 1))

            def iteration(it, first=False, tail=False, last=False):
                nxt = it + 1
                for u in range(4):
                    proj(it, 1, u)
                    if not first and u < LAG:
                        pv(it - 1, NST - LAG + u)
                    if u == 0:
                        max_transpose(it, 0)
                    for k in MAX1_BY_PROJ[u]:
                        max_chunk(it, 1, k)
                for u in range(4):
                    v_unit(it, u)
                    for k in MAX1_BY_V[u]:
                        max_chunk(it, 1, k)
                for s in range(NST):
                    scores(it, s)
                    if s == 0:
                        pair_ready(it, 1)
                    if s == LAG:
                        pe.wait_ge(v_lo, 8 * (it + 1))
                    if s in MAXT_AT and MAXT_AT[s] == 1:
                        max_transpose(it, 1)
                    if s in MAX_AT:
                        max_chunk(it, *MAX_AT[s])
                    if s in MAXT_AT and MAXT_AT[s] > 1:
                        max_transpose(it, MAXT_AT[s])
                    if s >= LAG:
                        pv(it, s - LAG)
                    if s in WO_AT and not first:
                        wo_unit(it - 1, WO_AT.index(s))
                    if not last:
                        if s in PROJ_AT:
                            proj(nxt, 0, PROJ_AT.index(s), y_at=4 * it, tail=tail)
                        if s in MAX_NEXT_AT:
                            if MAX_NEXT_AT[s] == 0:
                                pair_ready(nxt, 0)
                            max_chunk(nxt, 0, MAX_NEXT_AT[s])
                    if last:
                        tail_step(XTRA - 1, 0, s, LAST_A, NIT - 1)
                        tail_step(0, EXTRA, s, LAST_B, None)
                    elif tail:
                        tail_step(it - TAIL_LAG, 0, s, STEADY, it)

            for u in range(4):
                proj(0, 0, u, first=True)
            pe.wait_ge(const_b, 3)
            pe.wait_ge(buf_init, 14)
            pair_ready(0, 0)
            for k in range(NC):
                max_chunk(0, 0, k)
            iteration(0, first=True)
            with pe.Fori(1, TAIL_LAG) as it:
                iteration(it)
            with pe.Fori(TAIL_LAG, NIT - 1) as it:
                iteration(it, tail=True)
            iteration(NIT - 1, tail=True, last=True)
            for s in range(NST - LAG, NST):
                pv(NIT - 1, s)
            pe.wait_ge(tdve[0], ND * XTRA)
            for u in range(4):
                wo_unit(NIT - 1, u, alone=True)
            for g in range(NQ):
                t_transpose(finals(g), g, final=True)
            for r in range(3):
                for g in range(NQ):
                    t_up(finals(g), r, g)
                for g in range(NQ):
                    t_down(finals(g), r, g)

        @block.scalar
        def _(act):
            A = nc.scalar.activation

            def stage(nxt, p):
                act.wait_ge(raw_loaded, 16 * (4 * nxt + p + 1))
                if p == 0:
                    if started(4 * nxt):
                        act.wait_ge(v_mm, 4 * nxt)
                if p < KD:
                    A(xh[:, p, :], raw[:, :], ACT.Copy).then_inc(raw_hi, 1)
                else:
                    A(wh[:, p - KD, :], raw[:, 0:WC], ACT.Copy).then_inc(raw_hi, 1)

            def proj_evac(it, pair, u):
                c, kind = u % 2, u // 2
                act.wait_ge(proj_mm, 8 * it + 4 * pair + u + 1)
                used = NST * (it - 1) + 2 * NS * (pair + 1)
                if u == 0 and started(used):
                    act.wait_ge(st_mm, used)
                dst = (Q1, K1)[kind]
                sc = SCALE if kind == 0 else 1.0
                for hd, rows in ((0, slice(0, E)), (1, slice(E, P))):
                    A(dst[rows, 2 * pair + hd, CH * c:CH * c + CH], misc[u % 2][rows, :], ACT.Copy, scale=sc).then_inc(proj_hi, 1)

            def v_evac(it, u):
                act.wait_ge(v_mm, 4 * it + u + 1)
                if u == 0:
                    if started(NST * it):
                        act.wait_ge(pv_mm, NST * it)
                for t in range(2):
                    dst = VH[:, 2 * u + t, :, :].rearrange("p r (a e) -> p r a e", e=E)[:, :, 0:3:2, :]
                    src = misc[u % 2][:, 2 * P * t:2 * P * t + 2 * P].rearrange("p (r a e) -> p r a e", r=2, a=2)
                    A(dst, src, ACT.Copy).then_inc(v_hi, 1)

            def exp(it, s):
                i, c = STEPS[s % NS]
                o, _ = step_cols(i, c)
                if started(NST * it + s - 1):
                    act.wait_ge(*lo_of(it, s - 2))
                act.wait_ge(st_mm, NST * it + s + 1)
                A(pe_[:, s % 2, o:CH], stb[s % 2][:, o:CH], ACT.Exp).then_inc(exp_done, 1)
                if started(NST * it + s - RING + 1):
                    act.wait_ge(pv_mm, NST * it + s - RING + 1)
                A(ph[:, s % RING, o:CH], stb[s % 2][:, o:CH], ACT.Exp).then_inc(hi_done, 1)

            def copy_out(it, n, c):
                act.wait_ge(pv_mm, NST * it + NS * n + (4 if c == 0 else NS))
                if n < 2 and c == 0:
                    if started(4 * it):
                        act.wait_ge(wo_mm, 4 * it)
                if c == 0:
                    if started(16 * (QH * it + n - 1)):
                        act.wait_ge(sums_loaded, 16 * (QH * it + n - 1))
                rows, srow = (slice(0, E), E) if n % 2 == 0 else (slice(E, P), 0)
                cols = slice(CH * c, CH * c + CH)
                A(HT[rows, n // 2, cols], pvb[c][rows, :], ACT.Copy)
                A(rsum[srow:srow + 1, cols], pvb[c][srow:srow + 1, :], ACT.Copy).then_inc(ht_copied, 1)

            def t_x1(n, g=0):
                act.wait_ge(tpe[g], NPE * n + PEC["tr"])
                A(T[g].x1h[:, :, :], T[g].bk[0][:, :].rearrange("p (k n) -> p k n", k=KD), ACT.Copy).then_inc(tact[g], 1)

            def t_tanh(n, r, g=0):
                act.wait_ge(tpe[g], NPE * n + PEC[f"u{r}"])
                if r:
                    act.wait_ge(tpool[g], NP * n + PL[f"hl{r - 1}"])
                A(T[g].th[:, :, :], T[g].bk[0][:, :].rearrange("p (k n) -> p k n", k=2), ACT.Tanh,
                  scale=0.5 * WSCALE).then_inc(tact[g], 1)

            def tail_step(n, g, s, at):
                if s == at["X1S"]:
                    t_x1(n, g)
                if s in at["GATE"]:
                    t_tanh(n, at["GATE"].index(s), g)

            def iteration(it, first=False, tail=False, last=False):
                nxt = it + 1
                for u in range(4):
                    proj_evac(it, 1, u)
                if not first:
                    copy_out(it - 1, QH - 1, 1)
                for u in range(4):
                    v_evac(it, u)
                for s in range(NST):
                    if s - 1 in PROJ_AT and not last:
                        proj_evac(nxt, 0, PROJ_AT.index(s - 1))
                    if s in COPY_AT:
                        copy_out(it, *COPY_AT[s])
                    exp(it, s)
                    if not last:
                        if s in STAGE_AT:
                            stage(nxt, STAGE_AT.index(s))
                    if last:
                        tail_step(XTRA - 1, 0, s, LAST_A)
                        tail_step(0, EXTRA, s, LAST_B)
                    elif tail:
                        tail_step(it - TAIL_LAG, 0, s, STEADY)

            for p in range(4):
                stage(0, p)
            for u in range(4):
                proj_evac(0, 0, u)
            iteration(0, first=True)
            with act.Fori(1, TAIL_LAG) as it:
                iteration(it)
            with act.Fori(TAIL_LAG, NIT - 1) as it:
                iteration(it, tail=True)
            iteration(NIT - 1, tail=True, last=True)
            copy_out(NIT - 1, QH - 1, 1)
            for g in range(NQ):
                t_x1(finals(g), g)
            for r in range(3):
                for g in range(NQ):
                    t_tanh(finals(g), r, g)

        @block.vector
        def _(dve):
            V = nc.vector

            def proj_rest(it, pair, u):
                c, kind = u % 2, u // 2
                n = 16 * it + 8 * pair + 2 * u
                cols = slice(CH * c, CH * c + CH)
                for hd, rows in ((0, slice(0, E)), (1, slice(E, P))):
                    hx = 2 * pair + hd
                    dve.wait_ge(proj_hi, n + hd + 1)
                    if kind == 0:
                        V.scalar_tensor_tensor(Q2[rows, hx, cols], misc[u % 2][rows, :], SCALE,
                                               Q1[rows, hx, cols].bitcast(F32), ALU.mult, ALU.subtract).then_inc(proj_lo, 1)
                    else:
                        other = slice(E, P) if hd == 0 else slice(0, E)
                        V.tensor_tensor(K1[other, hx, cols], misc[u % 2][rows, :],
                                        K1[rows, hx, cols].bitcast(F32), ALU.subtract).then_inc(proj_lo, 1)

            def v_rest(it, u):
                dve.wait_ge(v_hi, 8 * it + 2 * u + 2)
                for t in range(2):
                    def part(X):
                        return X[:, 2 * u + t, :, :].rearrange("p r (a e) -> p r a e", e=E)[:, :, 0:3:2, :]
                    src = misc[u % 2][:, 2 * P * t:2 * P * t + 2 * P].rearrange("p (r a e) -> p r a e", r=2, a=2)
                    V.tensor_tensor(part(VL), src, part(VH).bitcast(F32), ALU.subtract).then_inc(v_lo, 1)

            def max_chunk(it, n, k):
                e = RING_AT["c", n, k]
                dve.wait_ge(mx_mm, NMX * it + e + 1)
                if k == 0:
                    if started(NMX * it + (RING_AT["t", n - 2, 0] + 1 if n >= 2 else 0)):
                        dve.wait_ge(mx_mm, NMX * it + (RING_AT["t", n - 2, 0] + 1 if n >= 2 else 0))
                j, c = CHUNKS[k]
                width = min(CH, P * (j + 1) - CH * c)
                at = j if c == 0 else TT + j - 4
                V.reduce_max(mp[:, n % 2, at:at + 1], mxb[e % 2][:, 0:width], AX.X).then_inc(mx_read, 1)
                if k == NC - 1:
                    dve.wait_ge(mx_read, NMX * it + e + 1)
                    V.tensor_tensor(mp[:, n % 2, 4:TT], mp[:, n % 2, 4:TT], mp[:, n % 2, TT:NC], ALU.max).then_inc(mx_comb, 1)

            def max_row8(it, n):
                e = RING_AT["t", n, 0]
                dve.wait_ge(mx_mm, NMX * it + e + 1)
                if n >= 2:
                    dve.wait_ge(max_row[n - 2], 16 * (it + 1))
                else:
                    if started(16 * it):
                        dve.wait_ge(max_row[n + 2], 16 * it)
                V.tensor_scalar(M8[:, n % 2, :], mxb[e % 2][0:TT, 0:P], -1.0, None, ALU.mult).then_inc(mx_read, 1)

            def probs_lo(it, s):
                i, c = STEPS[s % NS]
                o, _ = step_cols(i, c)
                dve.wait_ge(hi_done, NST * it + s + 1)
                V.tensor_tensor(pl[:, s % RING, o:CH], pe_[:, s % 2, o:CH], ph[:, s % RING, o:CH].bitcast(F32),
                                ALU.subtract).then_inc(lo_dve, 1)

            def recip(it, n):
                k = QH * it + n
                dve.wait_ge(sums_loaded, 16 * (k + 1))
                if started(16 * k):
                    dve.wait_ge(recip_stored, 16 * k)
                if started(2 * it + n // 2):
                    dve.wait_ge(ht_norm, 2 * it + n // 2)
                V.reciprocal(R64[:, :], S64[:, :]).then_inc(recip_done, 1)

            def y_add(wi, u, seq):
                dve.wait_ge(wo_mm, 4 * wi + u + 1)
                if u == 0:
                    dve.wait_ge(y_inited, 16 * (seq + 1))
                yy = y[:, 2 * u:2 * u + 2, :]
                V.tensor_tensor(yy, misc[u % 2][:, :].rearrange("p (t d) -> p t d", t=2), yy, ALU.add).then_inc(y_added, 1)

            def own(n, key, g):
                dve.wait_ge(tdve[g], ND * n + DV[key])

            def stats(n, x2, keys, g):
                for t in range(2):
                    V.bn_stats(T[g].st[:, t, :], x2[:, t, :]).then_inc(tdve[g], 1)
                own(n, keys[1], g)
                V.memset(carrier[:, :], 0.0)
                for t in range(2):
                    V.bn_aggr(T[g].mv[:, t, :], T[g].st[:, t, :]).then_inc(tdve[g], 1)

            def normalise(n, key, g=0, final=False):
                dve.wait_ge(tpool[g], NP * n + PL[key])
                x2 = rows_of(g, final)
                for t in range(2):
                    V.tensor_scalar(x2[:, t, :], x2[:, t, :], T[g].mv[:, t, 0:1], T[g].rs[:, t:t + 1], ALU.subtract, ALU.mult).then_inc(tdve[g], 1)

            def t_ln1(n, g=0, final=False):
                if final:
                    dve.wait_ge(y_added, 4 * (NIT - 1) + g + 1)
                else:
                    dve.wait_ge(tail_loaded[g], 32 * (n + 1))
                stats(n, rows_of(g, final), ["st1a", "st1b"], g)

            def t_add(n, g=0, final=False):
                dve.wait_ge(tpool[g], NP * n + PL["gam"])
                V.tensor_tensor(rows_of(g, final), rows_of(g, final), T[g].xt[:, :, :], ALU.add).then_inc(tdve[g], 1)
                own(n, "add", g)
                stats(n, rows_of(g, final), ["st2a", "st2b"], g)

            def t_x1lo(n, g=0):
                dve.wait_ge(tact[g], NA * n + AC["x1hi"])
                V.tensor_tensor(T[g].x1l[:, :, :], T[g].bk[0][:, :].rearrange("p (k n) -> p k n", k=KD),
                                T[g].x1h[:, :, :].bitcast(F32), ALU.subtract).then_inc(tdve[g], 1)

            def t_glu(n, r, g=0):
                dve.wait_ge(tact[g], NA * n + AC[f"tanh{r}"])
                V.scalar_tensor_tensor(T[g].th[:, :, :], T[g].th[:, :, :], 1.0, T[g].bk[0][:, :].rearrange("p (k n) -> p k n", k=2),
                                       ALU.add, ALU.mult).then_inc(tdve[g], 1)
                own(n, f"tg{r}", g)
                V.tensor_tensor(T[g].th[:, :, :], T[g].bk[1][:, :].rearrange("p (k n) -> p k n", k=2), T[g].th[:, :, :], ALU.mult).then_inc(tdve[g], 1)
                own(n, f"h{r}", g)
                V.tensor_copy(T[g].hh[:, :, :], T[g].th[:, :, :]).then_inc(tdve[g], 1)

            def t_y2(n, r, g=0, final=False):
                dve.wait_ge(tpe[g], NPE * n + PEC[f"d{r}"])
                if r:
                    own(n, f"y2{r - 1}", g)
                V.scalar_tensor_tensor(rows_of(g, final), T[g].bk[0][:, :].rearrange("p (t d) -> p t d", t=2), 0.5 * WSCALE ** 3,
                                       rows_of(g, final), ALU.mult, ALU.add).then_inc(tdve[g], 1)

            def t_ln3(n, g=0, final=False):
                own(n, "y22", g)
                stats(n, rows_of(g, final), ["st3a", "st3b"], g)

            def tail_y2(n, g, s, at):
                if s in at["Y2"]:
                    t_y2(n, at["Y2"].index(s), g)

            def tail_step(n, g, s, at):
                if s == at["LN1"]:
                    t_ln1(n, g)
                if s == at["LN1N"]:
                    normalise(n, "r1", g)
                if s == at["ADD"]:
                    t_add(n, g)
                if s == at["X1"]:
                    normalise(n, "r2", g)
                if s == at["X1S"]:
                    t_x1lo(n, g)
                if s in at["GATE"]:
                    t_glu(n, at["GATE"].index(s), g)
                if s == at["LN3"]:
                    t_ln3(n, g)
                if s == at["OUT"]:
                    normalise(n, "r3", g)

            def iteration(it, first=False, tail=False, last=False):
                nxt = it + 1
                for u in range(4):
                    proj_rest(it, 1, u)
                    if u == 0:
                        max_row8(it, 0)
                    for k in MAX1_BY_PROJ[u]:
                        max_chunk(it, 1, k)
                for u in range(4):
                    v_rest(it, u)
                    for k in MAX1_BY_V[u]:
                        max_chunk(it, 1, k)
                    if u == 1 and not first:
                        recip(it - 1, QH - 1)
                for s in range(NST):
                    if last:
                        tail_y2(XTRA - 1, 0, s, LAST_A)
                        tail_y2(0, EXTRA, s, LAST_B)
                    elif tail:
                        tail_y2(it - TAIL_LAG, 0, s, STEADY)
                    if s in MAXT_AT and MAXT_AT[s] == 1:
                        max_row8(it, 1)
                    if s in MAX_AT:
                        max_chunk(it, *MAX_AT[s])
                    if s in MAXT_AT and MAXT_AT[s] > 1:
                        max_row8(it, MAXT_AT[s])
                    if s in MAX_NEXT_AT and not last:
                        max_chunk(nxt, 0, MAX_NEXT_AT[s])
                    if s % LO_VECTOR == LO_VECTOR - 1:
                        probs_lo(it, s)
                    if s in RECIP_AT:
                        recip(it, RECIP_AT[s])
                    if s - 1 in WO_AT and not first:
                        y_add(it - 1, WO_AT.index(s - 1), (it - 1) // NQ)
                    if not last:
                        if s - 1 in PROJ_AT:
                            proj_rest(nxt, 0, PROJ_AT.index(s - 1))
                    if last:
                        tail_step(XTRA - 1, 0, s, LAST_A)
                        tail_step(0, EXTRA, s, LAST_B)
                    elif tail:
                        tail_step(it - TAIL_LAG, 0, s, STEADY)
                if last:
                    for s in range(NST, LAST_B["OUT"] + 1):
                        tail_y2(0, EXTRA, s, LAST_B)
                        tail_step(0, EXTRA, s, LAST_B)

            V.memset(VH[:, :, :, E:2 * E].bitcast(F32), 1.0).then_inc(buf_init, 1)
            V.memset(VL[:, :, :, E:2 * E].bitcast(F32), 0.0).then_inc(buf_init, 1)
            for pair in range(2):
                a, b = 2 * pair, 2 * pair + 1
                for X in (Q2, K2):
                    V.memset(X[E:P, a, :].bitcast(F32), 0.0).then_inc(buf_init, 1)
                    V.memset(X[0:E, b, :].bitcast(F32), 0.0).then_inc(buf_init, 1)
            dve.wait_ge(buf_init, 10)
            for pair in range(2):
                V.memset(K2[E:E + 1, 2 * pair, :].bitcast(F32), 1.0).then_inc(buf_init, 1)
                V.memset(K2[0:1, 2 * pair + 1, :].bitcast(F32), 1.0).then_inc(buf_init, 1)
            dve.wait_ge(const_step, 8)
            V.tensor_copy(maskT[:, :], mraw[:, 0:2 * P]).then_inc(const_b, 1)
            V.tensor_copy(maskS[:, :], mraw[:, 2 * P:3 * P]).then_inc(const_b, 1)
            V.tensor_copy(identb[:, :], identf[:, :]).then_inc(const_b, 1)
            for u in range(4):
                proj_rest(0, 0, u)
            for k in range(NC):
                max_chunk(0, 0, k)
            iteration(0, first=True)
            with dve.Fori(1, TAIL_LAG) as it:
                iteration(it)
            with dve.Fori(TAIL_LAG, NIT - 1) as it:
                iteration(it, tail=True)
            iteration(NIT - 1, tail=True, last=True)
            recip(NIT - 1, QH - 1)
            for g in range(NQ):
                y_add(NIT - 1, g, B - 1)
                t_ln1(finals(g), g, final=True)
            for g in range(NQ):
                normalise(finals(g), "r1", g, final=True)
            for g in range(NQ):
                t_add(finals(g), g, final=True)
            for g in range(NQ):
                normalise(finals(g), "r2", g, final=True)
            for g in range(NQ):
                t_x1lo(finals(g), g)
            for r in range(3):
                for g in range(NQ):
                    t_glu(finals(g), r, g)
                for g in range(NQ):
                    t_y2(finals(g), r, g, final=True)
            for g in range(NQ):
                t_ln3(finals(g), g, final=True)
            for g in range(NQ):
                normalise(finals(g), "r3", g, final=True)

        @block.gpsimd
        def _(pool):
            G = nc.gpsimd

            def stage(nxt, p):
                pool.wait_ge(raw_hi, 4 * nxt + p + 1)
                if p < KD:
                    G.tensor_tensor(xl[:, p, :], raw[:, :], xh[:, p, :].bitcast(F32), ALU.subtract).then_inc(raw_split, 1)
                else:
                    G.tensor_tensor(wl[:, p - KD, :], raw[:, 0:WC], wh[:, p - KD, :].bitcast(F32), ALU.subtract).then_inc(raw_split, 1)

            def probs_lo(it, s):
                i, c = STEPS[s % NS]
                o, _ = step_cols(i, c)
                pool.wait_ge(hi_done, NST * it + s + 1)
                G.tensor_tensor(pl[:, s % RING, o:CH], pe_[:, s % 2, o:CH], ph[:, s % RING, o:CH].bitcast(F32),
                                ALU.subtract).then_inc(lo_pool, 1)

            def norm(it, pair):
                pool.wait_ge(recip_bc, 16 * (QH * it + 2 * pair + 2))
                G.tensor_tensor(HT[:, pair, :], HT[:, pair, :], RB[:, :], ALU.mult).then_inc(ht_norm, 1)

            def own(n, key, g):
                pool.wait_ge(tpool[g], NP * n + PL[key])

            def rstd(n, eps, dkey, ekey, g=0):
                pool.wait_ge(tdve[g], ND * n + DV[dkey])
                G.tensor_tensor(T[g].rs, T[g].mv[:, :, 1:2].rearrange("p t o -> p (t o)"), eps[:, :], ALU.add).then_inc(tpool[g], 1)
                own(n, ekey, g)
                G.tensor_tensor(T[g].rs, T[g].rs, halves[:, :], ALU.pow).then_inc(tpool[g], 1)

            def over_rows(v):
                return v[:, :].rearrange("p (o d) -> p o d", o=1).broadcast_to([P, 2, D])

            def t_xb(n, g=0, loads=None):
                if loads is None:
                    loads = 32 * (n + 1)
                pool.wait_ge(tail_loaded[g], loads)
                pool.wait_ge(consts_loaded, 32)
                G.tensor_tensor(T[g].xt[:, :, :], T[g].xt[:, :, :], over_rows(bt), ALU.add).then_inc(tpool[g], 1)

            def t_gamma(n, g=0, final=False):
                pool.wait_ge(tdve[g], ND * n + DV["n1b"])
                G.tensor_tensor(rows_of(g, final), rows_of(g, final), over_rows(gm), ALU.mult).then_inc(tpool[g], 1)

            def t_hl(n, r, g=0):
                pool.wait_ge(tdve[g], ND * n + DV[f"hh{r}"])
                G.tensor_tensor(T[g].hl[:, :, :], T[g].th[:, :, :], T[g].hh[:, :, :].bitcast(F32), ALU.subtract).then_inc(tpool[g], 1)

            def tail_step(n, g, s, at):
                if s == at["LN1"]:
                    t_xb(n, g)
                if s == at["LN1R"]:
                    rstd(n, eps_attn, "mv1b", "e1", g)
                if s == at["AFF"]:
                    t_gamma(n, g)
                if s == at["LN2R"]:
                    rstd(n, eps_ln, "mv2b", "e2", g)
                if s in at["HS"]:
                    t_hl(n, at["HS"].index(s), g)
                if s == at["LN3R"]:
                    rstd(n, eps_ln, "mv3b", "e3", g)

            def iteration(it, first=False, tail=False, last=False):
                if not first:
                    norm(it - 1, 1)
                for s in range(NST):
                    if s % LO_VECTOR < LO_VECTOR - 1:
                        probs_lo(it, s)
                    if s in STAGE_AT and not last:
                        stage(it + 1, STAGE_AT.index(s))
                    if s == NORM_AT:
                        norm(it, 0)
                    if last:
                        tail_step(XTRA - 1, 0, s, LAST_A)
                        tail_step(0, EXTRA, s, LAST_B)
                    elif tail:
                        tail_step(it - TAIL_LAG, 0, s, STEADY)
                if last:
                    for s in range(NST, LAST_B["OUT"] + 1):
                        tail_step(0, EXTRA, s, LAST_B)

            G.memset(identf[:, :], 0.0).then_inc(const_step, 1)
            G.memset(mraw[:, :], 0.0).then_inc(const_step, 1)
            G.memset(halves[:, :], -0.5).then_inc(const_step, 1)
            G.memset(eps_attn[:, :], LN_EPS_ATTN).then_inc(const_step, 1)
            G.memset(eps_ln[:, :], LN_EPS).then_inc(const_step, 1)
            pool.wait_ge(const_step, 5)
            G.affine_select(out=identf[:, :], in_=identf[:, :], compare_op=ALU.not_equal, fill=1.0, base=0,
                            pattern=[[-1, P]], channel_multiplier=1).then_inc(const_step, 1)
            G.affine_select(out=mraw[:, 0:2 * P], in_=mraw[:, 0:2 * P], compare_op=ALU.is_ge, fill=MASKED, base=-P,
                            pattern=[[1, 2 * P]], channel_multiplier=-1).then_inc(const_step, 1)
            G.affine_select(out=mraw[:, 2 * P:3 * P], in_=mraw[:, 2 * P:3 * P], compare_op=ALU.is_ge, fill=MASKED, base=0,
                            pattern=[[-1, P]], channel_multiplier=1).then_inc(const_step, 1)
            for p in range(4):
                stage(0, p)
            for n, wt in enumerate((Wg, Wu, Wd)):
                pool.wait_ge(ffn_raw, 16 * (n + 1))
                dst = wt[:, :, :] if n < 2 else wt[:, :, :].rearrange("p (a b) d -> p a (b d)", a=2)
                G.tensor_copy(dst, HT[:, :, 0:HID].bitcast(I32)).then_inc(ffn_w, 1)
            iteration(0, first=True)
            with pool.Fori(1, TAIL_LAG) as it:
                iteration(it)
            with pool.Fori(TAIL_LAG, NIT - 1) as it:
                iteration(it, tail=True)
            iteration(NIT - 1, tail=True, last=True)
            norm(NIT - 1, 1)
            for g in range(NQ):
                t_xb(finals(g), g, loads=32 * finals(g) + 16)
            for g in range(NQ):
                rstd(finals(g), eps_attn, "mv1b", "e1", g)
            for g in range(NQ):
                t_gamma(finals(g), g, final=True)
            for g in range(NQ):
                rstd(finals(g), eps_ln, "mv2b", "e2", g)
            for r in range(3):
                for g in range(NQ):
                    t_hl(finals(g), r, g)
            for g in range(NQ):
                rstd(finals(g), eps_ln, "mv3b", "e3", g)


def kernel(L0_attn_x, L0_attn_Wq, L0_attn_Wk, L0_attn_Wv, L0_attn_Wo, L0_attn_gamma, L0_attn_beta,
           L0_ffn_w_gate, L0_ffn_w_up, L0_ffn_w_down):
    import numpy as np
    import concourse.bacc as bacc
    from concourse.bass_utils import run_bass_kernel_spmd as run

    x = np.ascontiguousarray(L0_attn_x)
    w3 = np.stack([np.asarray(a) for a in (L0_attn_Wq, L0_attn_Wk, L0_attn_Wv)])
    w3 = w3.reshape(3, NQ, QH, KD, P, E).transpose(1, 3, 4, 0, 2, 5).reshape(NQ, KD, P, 3 * QH * E)
    arrays = {
        "xT": x.transpose(0, 2, 1).reshape(B, KD, P, S),
        "x": x,
        "wqkv": w3,
        "wo": np.asarray(L0_attn_Wo).reshape(NQ, 2, P, D),
        "w_gate_T": np.asarray(L0_ffn_w_gate).T.reshape(KD, P, HID).transpose(1, 0, 2),
        "w_up_T": np.asarray(L0_ffn_w_up).T.reshape(KD, P, HID).transpose(1, 0, 2),
        "w_down_T": np.asarray(L0_ffn_w_down).T.reshape(NH6, P, D).transpose(1, 0, 2).reshape(P, 2, HID),
        "gamma": np.asarray(L0_attn_gamma).reshape(1, D),
        "beta": np.asarray(L0_attn_beta).reshape(1, D),
    }
    arrays = {k: np.ascontiguousarray(a) for k, a in arrays.items()}
    nc = bacc.Bacc("TRN2", target_bir_lowering=False, num_devices=1)
    aps = {k: nc.dram_tensor(k, a.shape, mybir.dt.from_np(a.dtype), kind="ExternalInput").ap() for k, a in arrays.items()}
    out = nc.dram_tensor("out", (B, S, D), F32, kind="ExternalOutput").ap()
    yscr = nc.dram_tensor("y_scratch", (S, D), F32, kind="Internal").ap()
    rscr = nc.dram_tensor("recip_scratch", (QH, S), F32, kind="Internal").ap()
    build(nc, aps["xT"], aps["x"], aps["wqkv"], aps["wo"], aps["w_gate_T"], aps["w_up_T"], aps["w_down_T"],
          aps["gamma"], aps["beta"], out, yscr, rscr)
    r = run(nc, [arrays], core_ids=[0])
    return r.results[0]["out"]
```
